# Optimizing a Trainium2 kernel written in Bass

```python
import numpy as np
import jax
import jax.numpy as jnp

def _softmax(x, axis=-1):
    return jax.nn.softmax(x, axis=axis)

def _gelu(x):
    return jax.nn.gelu(x, approximate=True)

def _silu(x):
    return jax.nn.silu(x)

def _sigmoid(x):
    return jax.nn.sigmoid(x)

def _layernorm(x, axis=-1, eps=1e-05):
    m = jnp.mean(x, axis=axis, keepdims=True)
    v = jnp.var(x, axis=axis, keepdims=True)
    return (x - m) / jnp.sqrt(v + eps)

def _scatter_add(tgt, idx, src, axis=0):
    return tgt.at[idx].add(src)

def _segment_sum(src, seg, n):
    return jax.ops.segment_sum(src, seg, n)
kernel_name = 'mk_adj_seq_d1_adj_r2_2ea9ba'

def setup_inputs(seed: int=0):
    np.random.seed(seed)
    _w = jnp.asarray

    def _rec_inputs():
        import jax
        import jax.numpy as jnp
        _gk = jax.random.key(seed)
        x = -0.0005207 + 1.001 * jax.random.normal(jax.random.fold_in(_gk, 1), (4096, 256), jnp.float32)
        _a = jax.random.bernoulli(jax.random.fold_in(_gk, 2), 0.000488281, (4096, 4096))
        _a = jnp.logical_or(_a, jnp.swapaxes(_a, -1, -2))
        _a = jnp.logical_or(_a, jnp.eye(4096, dtype=bool))
        adj = _a.astype(jnp.int32)
        return (x, adj)
    x, adj = _rec_inputs()

    def _L0_gnn_setup():
        import jax, jax.numpy as jnp
        import numpy as np
        D_MODEL = 256
        N_HEADS = 8
        D_K = D_MODEL // N_HEADS
        D_FF = 1024
        N = 2048
        EPS = 1e-05

        def _layer_norm(x, g, b):
            mu = jnp.mean(x, axis=-1, keepdims=True)
            var = jnp.mean(jnp.square(x - mu), axis=-1, keepdims=True)
            return (x - mu) * jax.lax.rsqrt(var + EPS) * g + b
        key = jax.random.key(seed)
        ks = jax.random.split(key, 16)
        s = 1.0 / np.sqrt(D_MODEL)
        sf = 1.0 / np.sqrt(D_FF)
        inp = {'h': jax.random.normal(ks[0], (N, D_MODEL), dtype=jnp.float32), 'adj': jax.random.randint(ks[1], (N, N), 0, 2, dtype=jnp.int32), 'Wq': jax.random.uniform(ks[2], (D_MODEL, D_MODEL), jnp.float32, -s, s), 'bq': jnp.zeros((D_MODEL,), jnp.float32), 'Wk': jax.random.uniform(ks[3], (D_MODEL, D_MODEL), jnp.float32, -s, s), 'bk': jnp.zeros((D_MODEL,), jnp.float32), 'Wv': jax.random.uniform(ks[4], (D_MODEL, D_MODEL), jnp.float32, -s, s), 'bv': jnp.zeros((D_MODEL,), jnp.float32), 'Wo': jax.random.uniform(ks[5], (D_MODEL, D_MODEL), jnp.float32, -s, s), 'bo': jnp.zeros((D_MODEL,), jnp.float32), 'W1': jax.random.uniform(ks[6], (D_FF, D_MODEL), jnp.float32, -s, s), 'b1': jnp.zeros((D_FF,), jnp.float32), 'W2': jax.random.uniform(ks[7], (D_MODEL, D_FF), jnp.float32, -sf, sf), 'b2': jnp.zeros((D_MODEL,), jnp.float32), 'ln1_g': jnp.ones((D_MODEL,), jnp.float32), 'ln1_b': jnp.zeros((D_MODEL,), jnp.float32), 'ln2_g': jnp.ones((D_MODEL,), jnp.float32), 'ln2_b': jnp.zeros((D_MODEL,), jnp.float32)}
        return inp
    _L0_gnn_all = _L0_gnn_setup()
    _L0_gnn_in = {k: v for k, v in _L0_gnn_all.items() if k in ('Wq', 'bq', 'Wk', 'bk', 'Wv', 'bv', 'Wo', 'bo', 'W1', 'b1', 'W2', 'b2', 'ln1_g', 'ln1_b', 'ln2_g', 'ln2_b')}
    del _L0_gnn_all
    return {'x': x, 'adj': adj, 'L0_gnn_Wq': _L0_gnn_in['Wq'], 'L0_gnn_bq': _L0_gnn_in['bq'], 'L0_gnn_Wk': _L0_gnn_in['Wk'], 'L0_gnn_bk': _L0_gnn_in['bk'], 'L0_gnn_Wv': _L0_gnn_in['Wv'], 'L0_gnn_bv': _L0_gnn_in['bv'], 'L0_gnn_Wo': _L0_gnn_in['Wo'], 'L0_gnn_bo': _L0_gnn_in['bo'], 'L0_gnn_W1': _L0_gnn_in['W1'], 'L0_gnn_b1': _L0_gnn_in['b1'], 'L0_gnn_W2': _L0_gnn_in['W2'], 'L0_gnn_b2': _L0_gnn_in['b2'], 'L0_gnn_ln1_g': _L0_gnn_in['ln1_g'], 'L0_gnn_ln1_b': _L0_gnn_in['ln1_b'], 'L0_gnn_ln2_g': _L0_gnn_in['ln2_g'], 'L0_gnn_ln2_b': _L0_gnn_in['ln2_b']}

def reference(x, adj, L0_gnn_Wq, L0_gnn_bq, L0_gnn_Wk, L0_gnn_bk, L0_gnn_Wv, L0_gnn_bv, L0_gnn_Wo, L0_gnn_bo, L0_gnn_W1, L0_gnn_b1, L0_gnn_W2, L0_gnn_b2, L0_gnn_ln1_g, L0_gnn_ln1_b, L0_gnn_ln2_g, L0_gnn_ln2_b):
    import jax
    import jax.numpy as jnp

    def _L0_gnn_ref(h, adj, Wq, bq, Wk, bk, Wv, bv, Wo, bo, W1, b1, W2, b2, ln1_g, ln1_b, ln2_g, ln2_b):
        import jax, jax.numpy as jnp
        import numpy as np
        D_MODEL = 256
        N_HEADS = 8
        D_K = D_MODEL // N_HEADS
        D_FF = 1024
        N = 2048
        EPS = 1e-05

        def _layer_norm(x, g, b):
            mu = jnp.mean(x, axis=-1, keepdims=True)
            var = jnp.mean(jnp.square(x - mu), axis=-1, keepdims=True)
            return (x - mu) * jax.lax.rsqrt(var + EPS) * g + b
        n = h.shape[0]
        mask = adj.astype(jnp.float32) + jnp.eye(n, dtype=jnp.float32)
        q = (h @ Wq.T + bq).reshape(n, N_HEADS, D_K)
        k = (h @ Wk.T + bk).reshape(n, N_HEADS, D_K)
        v = (h @ Wv.T + bv).reshape(n, N_HEADS, D_K)
        scores = jnp.einsum('nhd,mhd->hnm', q, k) / jnp.sqrt(jnp.float32(D_K))
        scores = jnp.where(mask[None, :, :] == 0, jnp.float32(-1000000000.0), scores)
        attn = jax.nn.softmax(scores, axis=-1)
        ctx = jnp.einsum('hnm,mhd->nhd', attn, v).reshape(n, D_MODEL)
        attn_out = ctx @ Wo.T + bo
        h1 = _layer_norm(h + attn_out, ln1_g, ln1_b)
        ff = jax.nn.relu(h1 @ W1.T + b1) @ W2.T + b2
        h2 = _layer_norm(h1 + ff, ln2_g, ln2_b)
        return h2
    x = _L0_gnn_ref(x, adj, L0_gnn_Wq, L0_gnn_bq, L0_gnn_Wk, L0_gnn_bk, L0_gnn_Wv, L0_gnn_bv, L0_gnn_Wo, L0_gnn_bo, L0_gnn_W1, L0_gnn_b1, L0_gnn_W2, L0_gnn_b2, L0_gnn_ln1_g, L0_gnn_ln1_b, L0_gnn_ln2_g, L0_gnn_ln2_b)
    return x

_drawn_inputs = setup_inputs


def setup_inputs(seed=0):
    import zlib

    import numpy as np

    out = dict(_drawn_inputs(seed))
    spreads = {'L0_gnn_bq': (0.0, 0.8),
     'L0_gnn_bk': (0.0, 0.8),
     'L0_gnn_bv': (0.0, 0.1),
     'L0_gnn_bo': (0.0, 0.1),
     'L0_gnn_b1': (0.0, 0.1),
     'L0_gnn_b2': (0.0, 0.1),
     'L0_gnn_ln1_g': (1.0, 0.2),
     'L0_gnn_ln1_b': (0.0, 0.1),
     'L0_gnn_ln2_g': (1.0, 0.2),
     'L0_gnn_ln2_b': (0.0, 0.1)}
    factors = {}
    for name, (base, spread) in spreads.items():
        noise = np.random.default_rng([zlib.crc32(name.encode()), seed]).standard_normal(out[name].shape)
        drawn = base * np.exp(spread * noise) if base else spread * noise
        out[name] = jnp.asarray(drawn.astype(out[name].dtype))
    for name, factor in factors.items():
        out[name] = (out[name] * factor).astype(out[name].dtype)
    return out
```

```python
import concourse.bass as bass
from concourse import mybir
from contextlib import ExitStack


def graph_attention_kernel(nc, x, xT, adj, wqT, wkT, wvT, woT, w1T, w2T,
                           bq, bk, bv, bo, b1, b2, ln1_g, ln1_b, ln2_g, ln2_b, out):
    fp32, bf16, i32, u32 = mybir.dt.float32, mybir.dt.bfloat16, mybir.dt.int32, mybir.dt.uint32
    ALU = mybir.AluOpType
    ACT = mybir.ActivationFunctionType
    AX = mybir.AxisListType

    N, D = x.shape
    F = w1T.shape[1]
    P = 128
    T = N // P
    H = 8
    DK = D // H
    KD = D // P
    KF = F // P
    GT = 4
    G = T // GT
    A = 16
    B = N // A
    S = 16
    R = 3
    C = 5
    E = C * P
    QB = 2 ** 8
    LB = (127 + 8) * B
    EXP_BITS = -(1 << 23)
    SCALE = float(DK) ** -0.5
    EPS = 1e-5
    PACK_LINKS = GT // 2 * 23
    LN_LINKS = 2
    SLOT_LINKS = 8
    TURN_LINKS = GT * (SLOT_LINKS + 2 * LN_LINKS)
    NA = S + 2

    kv_dram = nc.dram_tensor("kv_scratch", [N, 2 * D], fp32, kind="Internal").ap()
    kT_dram = nc.dram_tensor("kT_scratch", [D, N], fp32, kind="Internal").ap()
    xT_v = xT.rearrange("(k p) n -> p k n", p=P)

    ctx = ExitStack()
    with ctx:
        def sb(name, shape, dt=fp32):
            return ctx.enter_context(nc.sbuf_tensor(name, shape, dt))

        def sem(name):
            return ctx.enter_context(nc.semaphore(name))

        bank = [ctx.enter_context(nc.psum_tensor(f"bank{i}", [P, 512], fp32)) for i in range(8)]

        wq_sb = sb("wq_sb", [P, KD, D])
        wkv_sb = sb("wkv_sb", [P, KD, 2 * D])
        wo_sb = sb("wo_sb", [P, KD, D])
        w1_sb = sb("w1_sb", [P, KD, F])
        w2_sb = sb("w2_sb", [P, KF, D])
        bq_sb = sb("bq_sb", [P, D])
        bkv_sb = sb("bkv_sb", [P, 2 * D])
        bo_sb = sb("bo_sb", [P, D])
        b2_sb = sb("b2_sb", [P, D])
        g1_sb = sb("g1_sb", [P, D])
        be1_sb = sb("be1_sb", [P, D])
        g2_sb = sb("g2_sb", [P, D])
        be2_sb = sb("be2_sb", [P, D])
        b1_sb = sb("b1_sb", [P, KF])
        ident = sb("ident", [P, P])
        off_diag = sb("off_diag", [P, P], bf16)
        before = sb("before", [P, P])
        ones_col = sb("ones_col", [P, 1])
        bit_diag = sb("bit_diag", [P, A + 1, P], bf16)
        word_no = sb("word_no", [P, B], bf16)
        iota_e = sb("iota_e", [P, E])
        edge_no = sb("edge_no", [P, C])
        iota_s = sb("iota_s", [P, C, S])
        iota_q1 = sb("iota_q1", [P, P])
        neg_half = sb("neg_half", [P, 1])
        CONSTS = (A + 3) + 3 + 6
        QKV_IN, CONSTS_IN = 6 * 16, 10 * 16

        q_sb = sb("q_sb", [P, T, D])
        rows = sb("rows", [P, T, NA])
        deg = sb("deg", [P, T])
        last = sb("last", [P, T])
        minus_mid = sb("minus_mid", [P, T])
        reach = sb("reach", [P, T])
        row_sum = sb("row_sum", [P, T])
        diag = sb("diag", [P, T])
        bad = sb("bad", [P, 3, T])
        bad_col = sb("bad_col", [P, 1])
        bad_int = sb("bad_int", [1, 1], i32)

        adj_i_sb = sb("adj_i_sb", [P, 2, N], i32)
        adj_b_sb = sb("adj_b_sb", [P, 2, N], bf16)
        adj_i = [adj_i_sb[:, b, :] for b in range(2)]
        adj_b = [adj_b_sb[:, b, :] for b in range(2)]
        xT_sb = [sb(f"xT_sb{b}", [P, KD, P]) for b in range(2)]
        kv_out = [sb(f"kv_out{b}", [P, 2 * D]) for b in range(2)]
        diag_i = sb("diag_i", [P, T], i32)
        words = sb("words", [P, 2, S])
        words_left = [sb(f"words_left{b}", [P, B]) for b in range(2)]
        bits = sb("bits", [P, 2, R, S])
        rest = sb("rest", [P, R - 1, 2, S])
        words_i = sb("words_i", [P, 2, S], i32)
        word_at = sb("word_at", [P, 2, S], i32)
        codes = sb("codes", [P, 2, R, S], i32)
        found = sb("found", [P, 2, R, S])
        neighbours = sb("neighbours", [P, 2, S])
        found_left = sb("found_left", [P, 2, R * S])
        d_junk = sb("d_junk", [P, P])

        def region(first, words):
            return {"words": first, "at": 0, "size": words}

        def placed(where, name, words):
            at = where["at"]
            if at + words > where["size"]:
                return sb(name, [P, words])[:, :]
            where["at"] += words
            return where["words"][:, at:at + words]

        in_adj_b = region(adj_b_sb[:, :, :].rearrange("p b n -> p (b n)").bitcast(fp32), N)
        in_adj_i1 = region(adj_i[1].bitcast(fp32), N)
        in_xT = [region(xT_sb[b][:, :, :].rearrange("p k n -> p (k n)"), KD * P) for b in range(2)]
        in_kv_out = [region(kv_out[b][:, :], 2 * D) for b in range(2)]

        in_bit_diag = region(bit_diag[:, :, :].rearrange("p a n -> p (a n)")[:, 0:A * P].bitcast(fp32), A * P // 2)
        in_bkv = region(bkv_sb[:, :], 2 * D)

        edge_dist = placed(in_bit_diag, "edge_dist", E)
        KV = (C + 1) * 2 * D
        kv_e_sb = sb("kv_e_sb", [P, 2, C + 1, 2 * D])
        kv_e = [kv_e_sb[:, b, :, :] for b in range(2)] + [
            placed(where, name, KV).rearrange("p (c n) -> p c n", c=C + 1)
            for where, name in ((in_adj_b, "kv_e2"), (in_adj_i1, "kv_e3"))]
        row_to_edge = [sb(f"row_to_edge{b}", [P, E])[:, :] for b in range(2)] + [
            placed(where, name, E) for where, name in ((in_adj_b, "row_to_edge2"), (in_adj_i1, "row_to_edge3"))]
        edge_to_row = [sb(f"edge_to_row{b}", [P, C, P]) for b in range(2)]
        edge_row = [sb(f"edge_row{b}", [P, C]) for b in range(2)]
        slot = sb("slot", [P, C])
        slot_is = [sb(f"slot_is{j}", [P, C, S]) for j in range(GT)]
        nb_sel = sb("nb_sel", [P, C, S])
        nb_f = sb("nb_f", [P, C])
        nb_idx = [sb(f"nb_idx{b}", [P, C], u32) for b in range(2)]
        prod = sb("prod", [P, C + 1, D])
        score = sb("score", [P, C + 1, H])
        score_d = sb("score_d", [P, C, H])
        spread = sb("spread", [P, C, S, H])
        own = sb("own", [P, H])
        top_raw = sb("top_raw", [P, H])
        top = sb("top", [P, H])
        score_m = sb("score_m", [P, C, H])
        pv = sb("pv", [P, C + 1, D + H])
        ctx_acc = sb("ctx_acc", [P, D + H])
        inv_den = sb("inv_den", [P, H])

        att = sb("att", [P, GT, D])
        x_res = [sb(f"x_res{j}", [P, D]) for j in range(GT)]
        attT = placed(in_bit_diag, "attT", KD * P).rearrange("p (k n) -> p k n", k=KD)
        h_sum = [sb(f"h_sum{n}", [P, D]) for n in range(2)]
        stats = [sb(f"stats{n}", [P, 6]) for n in range(2)]
        mean_var = [sb(f"mean_var{n}", [P, 2]) for n in range(2)]
        rstd = [sb(f"rstd{n}", [P, 1]) for n in range(2)]
        shift = [sb(f"shift{n}", [P, 1]) for n in range(2)]
        h1 = [sb(f"h1_{j}", [P, D]) for j in range(GT)]
        h1_b2 = [placed(in_xT[j] if j < 2 else in_bkv, f"h1_b2_{j}", D) for j in range(GT)]
        h1T = sb("h1T", [P, KD, GT * P])
        HW = KF * GT * P
        hidden = adj_i_sb if 2 * N >= HW else sb("hidden", [P, 1, HW], i32)
        uT = hidden[:, :, :].rearrange("p b n -> p (b n)")[:, 0:HW].bitcast(fp32).rearrange("p (f n) -> p f n", f=KF)
        y = [placed(in_kv_out[j // 2], f"y{j}", D) for j in range(GT)]

        qkv_in = sem("qkv_in")
        consts_in = sem("consts_in")
        diag_in = sem("diag_in")
        ident_made = sem("ident_made")
        consts_made = sem("consts_made")
        adj_in = [sem(f"adj_in{b}") for b in range(2)]
        xT_in = [sem(f"xT_in{b}") for b in range(2)]
        qkv_ready = sem("qkv_ready")
        kv_ready = sem("kv_ready")
        q_ready = sem("q_ready")
        kv_stored = [sem(f"kv_stored{b}") for b in range(2)]
        adj_cast = sem("adj_cast")
        diag_cleared = sem("diag_cleared")
        words_ready = sem("words_ready")
        list_ready = sem("list_ready")
        dve_step = sem("dve_step")
        off_ready = sem("off_ready")
        bad_sum = sem("bad_sum")
        bad_rows = sem("bad_rows")
        deg_ready = sem("deg_ready")
        kv_cleared = sem("kv_cleared")
        flag_ready = sem("flag_ready")
        spans_ready = sem("spans_ready")
        dist_ready = sem("dist_ready")
        rte_ready = sem("rte_ready")
        edge_rows_ready = sem("edge_rows_ready")
        edge_rows_read = sem("edge_rows_read")
        nb_ready = sem("nb_ready")
        etr_ready = sem("etr_ready")
        nb_in = [[sem(f"nb_in{j}_{c}") for c in range(C)] for j in range(GT)]
        own_in = [sem(f"own_in{j}") for j in range(GT)]
        q_edges = sem("q_edges")
        q_edges_read = sem("q_edges_read")
        own_score = sem("own_score")
        own_spread = sem("own_spread")
        slots_ready = sem("slots_ready")
        slots_filled = sem("slots_filled")
        top_ready = sem("top_ready")
        top_spread = sem("top_spread")
        shifted = sem("shifted")
        weights_ready = sem("weights_ready")
        pv_ready = sem("pv_ready")
        ctx_summed = sem("ctx_summed")
        att_ready = sem("att_ready")
        x_in = [sem(f"x_in{j}") for j in range(GT)]
        attT_ps = sem("attT_ps")
        attT_ready = sem("attT_ready")
        proj_ready = sem("proj_ready")
        x_bo_ready = sem("x_bo_ready")
        res_added = sem("res_added")
        var_ready = [sem(f"var{n}_ready") for n in range(2)]
        rstd_made = [sem(f"rstd{n}_made") for n in range(2)]
        rstd_ready = [sem(f"rstd{n}_ready") for n in range(2)]
        normed = [sem(f"normed{n}") for n in range(2)]
        gained = [sem(f"gained{n}") for n in range(2)]
        h1_ready = sem("h1_ready")
        h1_b2_ready = sem("h1_b2_ready")
        h1T_ps = sem("h1T_ps")
        h1T_ready = sem("h1T_ready")
        ff1_ready = sem("ff1_ready")
        hidden_ready = sem("hidden_ready")
        ff2_ready = sem("ff2_ready")
        ff2_read = sem("ff2_read")
        y_ready = sem("y_ready")
        y_out = [sem(f"y_out{j}") for j in range(GT)]
        free_made = sem("free_made")
        k_rows_in = sem("k_rows_in")
        kT_ps = sem("kT_ps")
        kT_copied = sem("kT_copied")
        kT_stored = sem("kT_stored")
        mask_in = sem("mask_in")
        mask_ready = sem("mask_ready")
        head_free = sem("head_free")
        head_in = sem("head_in")
        head_q = sem("head_q")
        qT_ps = sem("qT_ps")
        qT_ready = sem("qT_ready")
        scores_ps = sem("scores_ps")
        scores_kept = sem("scores_kept")
        shift_ready = sem("shift_ready")
        probs_ready = sem("probs_ready")
        pT_ps = sem("pT_ps")
        pT_ready = sem("pT_ready")
        head_summed = sem("head_summed")
        dense_step = sem("dense_step")
        mask_step = sem("mask_step")

        SC = 512
        NS = N // SC
        M4 = T // 4
        d_mask = adj_i[1]
        d_score = adj_b_sb[:, :, :].rearrange("p b n -> p (b n)").bitcast(fp32)
        kv_flat = kv_e_sb[:, :, :, :].rearrange("p b c n -> p (b c n)")
        d_k_rows = kv_flat[:, 0:D]
        d_kT_out = kv_flat[:, D:D + KD * P].rearrange("p (k n) -> p k n", k=KD)
        d_kT = kv_flat[0:DK, 0:N]
        d_v = prod[:, :, :].rearrange("p c n -> p (c n)")[:, 0:T * DK].rearrange("p (c d) -> p c d", c=T)
        pv_flat = pv[:, :, :].rearrange("p c n -> p (c n)")
        d_pT = [pv_flat[:, b * 512:(b + 1) * 512] for b in range(2)]
        d_q = ctx_acc[:, 0:DK]
        d_qT = spread[0:DK, 0, :, :].rearrange("p s h -> p (s h)")
        d_den, d_max, d_shift, d_inv = (inv_den[:, c:c + 1] for c in range(4))

        block = ctx.enter_context(nc.Block())

        def wait(eng, signal, value):
            if not isinstance(value, int) or value > 0:
                eng.wait_ge(signal, value)

        def settled_wait(eng, signal, value):
            if isinstance(value, int):
                wait(eng, signal, value)
                return
            with eng.register() as count:
                eng.reg_mov(count, value)
                eng.wait_ge(consts_made, CONSTS)
                eng.wait_ge(signal, count)

        def counter():
            return {"done": 0, "turn": None, "first": 0, "per_turn": 0, "here": 0}

        def enter(count, turn, first, per_turn):
            count["turn"], count["first"], count["per_turn"], count["here"] = turn, first, per_turn, 0

        def leave(count, turns):
            assert count["here"] == count["per_turn"], count["here"]
            count["done"] += turns * count["per_turn"]
            count["turn"] = None

        def raised(count):
            if count["turn"] is None:
                count["done"] += 1
                return count["done"]
            count["here"] += 1
            return (count["turn"] - count["first"]) * count["per_turn"] + (count["done"] + count["here"])

        def turns(eng, body, count, *chains):
            body(0)
            with eng.Fori(1, count - 1) as turn:
                for c in chains:
                    enter(c, turn, 1, PACK_LINKS)
                body(turn)
            for c in chains:
                leave(c, count - 2)
            body(count - 1)

        def exists(t):
            return not isinstance(t, int) or 0 <= t < T

        def run_slots(eng, slot, *chains):
            for j in range(GT - 2, GT):
                slot(-1, j)
            for turn in range(2):
                for j in range(GT):
                    slot(turn, j)
            if G > 3:
                with eng.Fori(2, G - 1) as turn:
                    for c in chains:
                        enter(c, turn, 2, TURN_LINKS)
                    for j in range(GT):
                        slot(turn, j)
                for c in chains:
                    leave(c, G - 3)
            for turn in range(G - 1, G + 1):
                for j in range(GT):
                    slot(turn, j)
            for j in range(GT - 1):
                slot(G + 1, j)

        def if_dense(eng, run):
            eng.wait_ge(flag_ready, 1)
            flag = eng.value_load(bad_int[0:1, 0:1], min_val=0, max_val=1)
            with eng.If(flag > 0):
                run()

        @block.sync
        def _(sp):
            def tile_in(t, b):
                sp.dma_start(adj_i[b], adj[bass.ds(t * P, P), :]).then_inc(adj_in[b], 16)

            def input_in(t, b):
                sp.dma_start(xT_sb[b][:, :, :], xT_v[:, :, bass.ds(t * P, P)]).then_inc(xT_in[b], 16)

            def weights_in(signal, *pairs):
                for dst, w in pairs:
                    sp.dma_start(dst, w.rearrange("(k p) n -> p k n", p=P)).then_inc(signal, 16)

            def vectors_in(signal, *pairs):
                for dst, v in pairs:
                    sp.dma_start(dst, v.partition_broadcast(P)).then_inc(signal, 16)

            tile_in(0, 0)
            weights_in(qkv_in, (wkv_sb[:, :, 0:D], wkT), (wkv_sb[:, :, D:2 * D], wvT), (wq_sb[:, :, :], wqT))
            vectors_in(qkv_in, (bq_sb[:, :], bq), (bkv_sb[:, 0:D], bk), (bkv_sb[:, D:2 * D], bv))
            input_in(0, 0)
            tile_in(1, 1)
            input_in(1, 1)
            weights_in(consts_in, (wo_sb[:, :, :], woT), (w1_sb[:, :, :], w1T), (w2_sb[:, :, :], w2T))
            vectors_in(consts_in, (bo_sb[:, :], bo), (b2_sb[:, :], b2), (g1_sb[:, :], ln1_g), (be1_sb[:, :], ln1_b),
                       (g2_sb[:, :], ln2_g), (be2_sb[:, :], ln2_b))
            with nc.allow_non_contiguous_dma(reason="a thousand words, and the diagonal's four thousand, once"):
                sp.dma_start(b1_sb[:, :], b1.rearrange("(k p) -> p k", p=P)).then_inc(consts_in, 16)
                sp.dma_start(diag_i[:, :], adj.rearrange("r c -> (r c)")[0:N * N:N + 1].rearrange("(t p) -> p t", p=P))\
                  .then_inc(diag_in, 16)

            def pack_turn(i):
                for j in range(GT):
                    t, b = i * GT + j, j % 2
                    if not (isinstance(t, int) and t + 2 >= T):
                        settled_wait(sp, adj_cast, t + 1)
                        tile_in(t + 2, b)
                        settled_wait(sp, qkv_ready, t + 1)
                        input_in(t + 2, b)
                    settled_wait(sp, kv_ready, t + 1)
                    sp.dma_start(kv_dram[bass.ds(t * P, P), :], kv_out[b][:, :]).then_inc(kv_stored[b], 16)

            turns(sp, pack_turn, T // GT)
            for b in range(2):
                sp.wait_ge(kv_stored[b], 16 * (T // 2))
            sp.wait_ge(kv_cleared, 3)

            def own_rows(t, turn, j):
                settled_wait(sp, pv_ready, t - 3)
                sp.dma_start(kv_e[j][:, C, :], kv_dram[bass.ds(t * P, P), :]).then_inc(own_in[j], 16)

            def residual(n, j, row0):
                settled_wait(sp, res_added, n - 3)
                sp.dma_start(x_res[j][:, :], x[bass.ds(row0, P), :]).then_inc(x_in[j], 16)

            def store(u, k, row0):
                settled_wait(sp, y_ready, u * GT + (k + 1))
                sp.dma_start(out[bass.ds(row0, P), :], y[k]).then_inc(y_out[k], 16)

            def slot(turn, j):
                s = turn * GT + j
                if exists(s + 2):
                    own_rows(s + 2, turn, (j + 2) % GT)
                if exists(s):
                    residual(s, j, s * P)
                for k in ((0,), (1, 2), (3,), ())[j]:
                    if exists((turn - 2) * GT):
                        store(turn - 2, k, (turn - 2) * (GT * P) + k * P)

            run_slots(sp, slot)

            def dense():
                settled_wait(sp, free_made, 1)
                with sp.Fori(0, T) as m:
                    settled_wait(sp, kT_copied, m + 1)
                    sp.dma_start(d_k_rows, kv_dram[bass.ds(m * P, P), 0:D]).then_inc(k_rows_in, 16)
                    settled_wait(sp, kT_copied, m + 2)
                    sp.dma_start(kT_dram.rearrange("(k p) n -> p k n", p=P)[:, :, bass.ds(m * P, P)],
                                 d_kT_out).then_inc(kT_stored, 16)
                    settled_wait(sp, kT_stored, m * 16 + 16)
                with sp.Fori(0, G) as g:
                    for k in range(GT):
                        residual((g + G) * GT + k, k, g * (GT * P) + k * P)
                    with sp.Fori(0, GT) as j:
                        settled_wait(sp, head_free, (g * GT + j) * H + 1)
                        sp.dma_start(d_mask, adj[bass.ds((g * GT + j) * P, P), :]).then_inc(mask_in, 16)
                        with sp.Fori(0, H) as h:
                            settled_wait(sp, head_free, (g * GT + j) * H + h + 1)
                            sp.dma_start(d_kT, kT_dram[bass.ds(h * DK, DK), :]).then_inc(head_in, 16)
                            sp.dma_start(d_v, kv_dram[:, bass.ds(h * DK + D, DK)].rearrange("(c p) d -> p c d", p=P))\
                              .then_inc(head_in, 16)
                    for k in range(GT):
                        store(g + G, k, g * (GT * P) + k * P)
                for k in range(GT):
                    sp.wait_ge(y_out[k], 32 * G)

            if_dense(sp, dense)
            for k in range(GT):
                sp.wait_ge(y_out[k], 16 * G)

        @block.gpsimd
        def _(pool):
            filled = [0]

            def diagonal(m, off, on):
                nc.gpsimd.memset(m, off).then_inc(ident_made, 1)
                filled[0] += 1
                pool.wait_ge(ident_made, filled[0])
                return nc.gpsimd.affine_select(out=m, in_=m, compare_op=ALU.not_equal, fill=on, base=0,
                                               pattern=[[-1, P]], channel_multiplier=1)
            for a in range(A):
                diagonal(bit_diag[:, a, :], 0.0, float(QB * 2 ** a)).then_inc(consts_made, 1)
            diagonal(bit_diag[:, A, :], 0.0, 1.0).then_inc(consts_made, 1)
            diagonal(off_diag[:, :], 1.0, 0.0).then_inc(consts_made, 1)
            diagonal(ident[:, :], 0.0, 1.0).then_inc(consts_made, 1)
            nc.gpsimd.memset(before[:, :], 1.0).then_inc(ident_made, 1)
            pool.wait_ge(ident_made, filled[0] + 1)
            nc.gpsimd.affine_select(out=before[:, :], in_=before[:, :], compare_op=ALU.is_gt, fill=0.0, base=0,
                                    pattern=[[1, P]], channel_multiplier=-1).then_inc(consts_made, 1)
            nc.gpsimd.memset(ones_col[:, :], 1.0).then_inc(consts_made, 1)
            nc.gpsimd.memset(neg_half[:, :], -0.5).then_inc(consts_made, 1)
            for m, pattern, base, per_partition in ((word_no[:, :], [[-1, B]], B - 1, 0), (iota_e[:, :], [[1, E]], 0, 0),
                                                    (edge_no[:, :], [[P, C]], 0, 1), (iota_s[:, :, :], [[0, C], [1, S]], 0, 0),
                                                    (iota_q1[:, :], [[1, P]], 1, 0), (rows[:, :, 0], [[0, T]], 1, 1)):
                nc.gpsimd.iota(m, pattern, base=base, channel_multiplier=per_partition,
                               allow_small_or_imprecise_dtypes=True).then_inc(consts_made, 1)
            nc.gpsimd.memset(kv_e_sb[:, :, :, :], 0.0).then_inc(kv_cleared, 1)
            pool.wait_ge(consts_in, CONSTS_IN)
            pool.wait_ge(words_ready, T)
            pool.wait_ge(diag_cleared, T)
            for j in (2, 3):
                nc.gpsimd.memset(kv_e[j], 0.0).then_inc(kv_cleared, 1)
            pool.wait_ge(kv_cleared, 3)
            for b in range(2):
                pool.wait_ge(kv_stored[b], 16 * (T // 2))

            def gather(t, j):
                settled_wait(pool, nb_ready, t + 1)
                settled_wait(pool, pv_ready, t - 3)
                for c in range(C):
                    pool.indirect_dma_start(kv_e[j][:, c, :], None, kv_dram,
                                            bass.IndirectOffsetOnAxis(nb_idx[j % 2][:, c:c + 1], 0),
                                            bounds_check=N - 1, oob_is_err=False).then_inc(nb_in[j][c], 16)

            def inverse_root(ln, n):
                pool.wait_ge(var_ready[ln], n + 1)
                nc.gpsimd.tensor_tensor(rstd[ln][:, :], mean_var[ln][:, 1:2], neg_half[:, :], ALU.pow)\
                  .then_inc(rstd_made[ln], 1)
                pool.wait_ge(rstd_made[ln], n + 1)
                nc.gpsimd.tensor_tensor(shift[ln][:, :], mean_var[ln][:, 0:1], rstd[ln][:, :], ALU.mult)\
                  .then_inc(rstd_ready[ln], 1)

            def gain_shift(ln, n, gain, bias, dst):
                pool.wait_ge(normed[ln], n + 1)
                nc.gpsimd.tensor_tensor(h_sum[ln][:, :], h_sum[ln][:, :], gain[:, :], ALU.mult).then_inc(gained[ln], 1)
                pool.wait_ge(gained[ln], n + 1)
                return nc.gpsimd.tensor_tensor(dst, h_sum[ln][:, :], bias[:, :], ALU.add)

            def residual_bias(n, turn, j):
                pool.wait_ge(x_in[j], turn * 16 + 16)
                nc.gpsimd.tensor_tensor(x_res[j][:, :], x_res[j][:, :], bo_sb[:, :], ALU.add).then_inc(x_bo_ready, 1)

            def h1_bias(u, k):
                pool.wait_ge(h1_ready, u * GT + (k + 1))
                wait(pool, ff2_read, (u - 1) * GT + (k + 1))
                nc.gpsimd.tensor_tensor(h1_b2[k], h1[k][:, :], b2_sb[:, :], ALU.add).then_inc(h1_b2_ready, 1)

            def second_norm(u, k):
                inverse_root(1, u * GT + k)
                wait(pool, y_out[k], u * 16)
                gain_shift(1, u * GT + k, g2_sb, be2_sb, y[k]).then_inc(y_ready, 1)

            def slot(turn, j):
                s = turn * GT + j
                if exists((turn - 2) * GT) and j < 2:
                    second_norm(turn - 2, 2 * j + 1)
                if exists(s - 1):
                    inverse_root(0, s - 1)
                if exists(s):
                    residual_bias(s, turn, j)
                if exists(s - 1):
                    wait(pool, h1T_ps, (turn - 1 + (j > 0)) * KD)
                    wait(pool, h1_b2_ready, s - 4)
                    gain_shift(0, s - 1, g1_sb, be1_sb, h1[(j - 1) % GT][:, :]).then_inc(h1_ready, 1)
                if exists((turn - 2) * GT) and j == 0:
                    second_norm(turn - 2, 2)
                if exists((turn - 1) * GT) and j == 3:
                    second_norm(turn - 1, 0)
                if exists(s + 2):
                    gather(s + 2, (j + 2) % GT)
                if exists((turn - 1) * GT) and j < 2:
                    for k in (2 * j, 2 * j + 1):
                        h1_bias(turn - 1, k)

            run_slots(pool, slot)

            def dense():
                with pool.Fori(0, G) as g:
                    u = g + G
                    for k in range(GT):
                        n = u * GT + k
                        residual_bias(n, u, k)
                        inverse_root(0, n)
                        gain_shift(0, n, g1_sb, be1_sb, h1[k][:, :]).then_inc(h1_ready, 1)
                    for k in range(GT):
                        h1_bias(u, k)
                    for k in range(GT):
                        second_norm(u, k)

            if_dense(pool, dense)

        @block.scalar
        def _(act):
            def pack_turn(i):
                for j in range(GT):
                    t, b = i * GT + j, j % 2
                    act.wait_ge(adj_in[b], (i * 2 + j // 2) * 16 + 16)
                    wait(act, words_ready, t - 1)
                    nc.scalar.activation(adj_b[b], adj_i[b], ACT.Square,
                                         accum_out=row_sum[:, bass.ds(t, 1)]).then_inc(adj_cast, 1)

            turns(act, pack_turn, T // GT)

            def weigh(t):
                act.wait_ge(shifted, t + 1)
                wait(act, ctx_summed, t)
                nc.scalar.activation(pv[:, 0:C, D:D + H], score_m[:, :, :], ACT.Exp, scale=SCALE)
                nc.scalar.activation(pv[:, C, D:D + H], top[:, :], ACT.Exp, scale=-SCALE).then_inc(weights_ready, 1)

            def distance(t):
                settled_wait(act, spans_ready, 1)
                settled_wait(act, rte_ready, t)
                nc.scalar.activation(edge_dist, iota_e[:, :], ACT.Square,
                                     bias=minus_mid[:, bass.ds(t, 1)]).then_inc(dist_ready, 1)

            def copy_att(n):
                act.wait_ge(attT_ps, n + 1)
                nc.scalar.activation(attT[:, :, :].rearrange("p k n -> p (k n)"), bank[6][:, 0:KD * P],
                                     ACT.Copy).then_inc(attT_ready, 1)

            def norm(ln, n):
                act.wait_ge(rstd_ready[ln], n + 1)
                nc.scalar.activation(h_sum[ln][:, :], h_sum[ln][:, :], ACT.Identity, bias=shift[ln][:, :],
                                     scale=rstd[ln][:, :]).then_inc(normed[ln], 1)

            def copy_h1(u, k):
                act.wait_ge(h1T_ps, u * KD + (k + 1))
                nc.scalar.activation(h1T[:, k, :], bank[6][:, :], ACT.Copy).then_inc(h1T_ready, 1)

            def relu(u, f):
                act.wait_ge(ff1_ready, u * KF + (f + 1))
                nc.scalar.activation(uT[:, f, :], bank[6 + f % 2][:, :], ACT.Relu,
                                     bias=b1_sb[:, f:f + 1]).then_inc(hidden_ready, 1)

            distance(0)

            def slot(turn, j):
                s = turn * GT + j
                if exists((turn - 1) * GT) and j == 1:
                    copy_h1(turn - 1, 1)
                if exists(s - 1):
                    copy_att(s - 1)
                if exists((turn - 2) * GT) and j < 2:
                    norm(1, (turn - 2) * GT + (2 * j + 1))
                if exists((turn - 1) * GT) and j in (1, 2):
                    relu(turn - 1, (j - 1) * 4)
                if exists(s - 1):
                    norm(0, s - 1)
                if exists((turn - 2) * GT) and j == 0:
                    norm(1, (turn - 2) * GT + 2)
                if exists((turn - 1) * GT) and j == 3:
                    norm(1, (turn - 1) * GT)
                if exists(s):
                    weigh(s)
                if exists(s + 3):
                    distance(s + 3)
                if exists((turn - 1) * GT) and j in (1, 2):
                    for i in range(1, 4):
                        relu(turn - 1, (j - 1) * 4 + i)
                if exists((turn - 1) * GT) and j == 0:
                    copy_h1(turn - 1, 0)

            run_slots(act, slot)

            def dense():
                with act.Fori(0, G) as g:
                    with act.Fori(0, GT) as j:
                        with act.Fori(0, H) as h:
                            n = (g * GT + j) * H + h
                            act.wait_ge(shift_ready, n + 1)
                            nc.scalar.activation(d_score, d_score, ACT.Exp, bias=d_shift, scale=SCALE,
                                                 accum_out=d_den).then_inc(probs_ready, 1)
                            for m in range(M4):
                                act.wait_ge(pT_ps, n * M4 + (m + 1))
                                nc.scalar.activation(d_pT[m % 2], bank[m % 2][:, :], ACT.Copy).then_inc(pT_ready, 1)
                    u = g + G
                    for k in range(GT):
                        copy_att(u * GT + k)
                        norm(0, u * GT + k)
                    for k in range(KD):
                        copy_h1(u, k)
                    for f in range(KF):
                        relu(u, f)
                    for k in range(GT):
                        norm(1, u * GT + k)

            if_dense(act, dense)

        @block.vector
        def _(dve):
            steps = counter()

            def link(ins, settled=False):
                ins.then_inc(dve_step, 1)
                (settled_wait if settled else wait)(dve, dve_step, raised(steps))

            dve.wait_ge(qkv_in, QKV_IN)
            dve.wait_ge(consts_made, CONSTS)

            def pack(t, b, stored):
                dve.wait_ge(qkv_ready, t + 1)
                wait(dve, kv_stored[b], stored)
                nc.vector.tensor_tensor(kv_out[b][:, :], bank[b][:, :], bkv_sb[:, :], ALU.add).then_inc(kv_ready, 1)
                nc.vector.tensor_tensor(q_sb[:, bass.ds(t, 1), :].rearrange("p o n -> p (o n)"), bank[2 + b][:, 0:D],
                                        bq_sb[:, :], ALU.add).then_inc(q_ready, 1)
                dve.wait_ge(adj_cast, t + 1)
                nc.vector.tensor_tensor(adj_b[b][:, bass.ds(t * P, P)], adj_b[b][:, bass.ds(t * P, P)], off_diag[:, :],
                                        ALU.mult).then_inc(diag_cleared, 1)

            def list_rows(t, j):
                settled_wait(dve, words_ready, t + 2)
                packed = [bank[4 + j + i][:, 0:B] for i in range(2)]
                for i in range(2):
                    link(nc.vector.max(words[:, i, 0:8], packed[i]), settled=True)
                for i in range(2):
                    link(nc.vector.match_replace(out=words_left[i][:, :], in_to_replace=words[:, i, 0:8],
                                                 in_values=packed[i], imm_value=0.0), settled=True)
                for i in range(2):
                    link(nc.vector.max(words[:, i, 8:16], words_left[i][:, :]), settled=True)
                left = words[:, :, :]
                for r in range(R):
                    link(nc.vector.tensor_scalar(bits[:, :, r, :].bitcast(i32), left.bitcast(i32), EXP_BITS, None,
                                                 ALU.bitwise_and))
                    if r < R - 1:
                        link(nc.vector.tensor_tensor(rest[:, r, :, :], left, bits[:, :, r, :], ALU.subtract))
                        left = rest[:, r, :, :]
                link(nc.vector.tensor_copy(words_i[:, :, :], words[:, :, :]))
                link(nc.vector.tensor_scalar(word_at[:, :, :], words_i[:, :, :], QB - 1, None, ALU.bitwise_and))
                link(nc.vector.tensor_scalar(codes[:, :, :, :], bits[:, :, :, :].bitcast(i32), 23, None,
                                             ALU.arith_shift_right))
                for i in range(2):
                    link(nc.vector.scalar_tensor_tensor(found[:, i, :, :], codes[:, i, :, :], float(B),
                                                        word_at[:, i, :].unsqueeze(1).to_broadcast([P, R, S]),
                                                        ALU.mult, ALU.add), settled=True)
                candidates = [found[:, i, :, :].rearrange("p r s -> p (r s)") for i in range(2)]
                for i in range(2):
                    link(nc.vector.max(neighbours[:, i, 0:8], candidates[i]), settled=True)
                for i in range(2):
                    link(nc.vector.match_replace(out=found_left[:, i, :], in_to_replace=neighbours[:, i, 0:8],
                                                 in_values=candidates[i], imm_value=0.0), settled=True)
                for i in range(2):
                    link(nc.vector.max(neighbours[:, i, 8:16], found_left[:, i, :]), settled=True)
                link(nc.vector.tensor_copy(rows[:, bass.ds(t, 2), 2:NA], neighbours[:, :, :]), settled=True)

            def pack_turn(i):
                for j in range(0, GT, 2):
                    t = i * GT + j
                    for b in range(2):
                        pack(t + b, b, (i * 2 + j // 2) * 16)
                    if not (isinstance(t, int) and t == 0):
                        list_rows(t - 2, (j - 2) % GT)

            turns(dve, pack_turn, T // GT, steps)
            list_rows(T - 2, GT - 2)

            dve.wait_ge(diag_in, 16)
            dve.wait_ge(consts_in, CONSTS_IN)
            link(nc.vector.tensor_copy(diag[:, :], diag_i[:, :]))
            listed = adj_i_sb[:, 0, 0:T * S].bitcast(fp32).rearrange("p (t s) -> p t s", t=T)
            link(nc.vector.tensor_scalar(listed, rows[:, :, 2:NA], float(LB), None, ALU.is_ge))
            link(nc.vector.tensor_reduce(deg[:, :], listed, AX.X, ALU.add))
            nc.vector.tensor_copy(deg[:, 0:1], deg[:, 0:1]).then_inc(deg_ready, 1)
            link(nc.vector.tensor_tensor(bad[:, 0, :], row_sum[:, :], diag[:, :], ALU.subtract))
            link(nc.vector.tensor_tensor(bad[:, 0, :], bad[:, 0, :], deg[:, :], ALU.not_equal))
            link(nc.vector.scalar_tensor_tensor(bad[:, 1, :], diag[:, :], -1.0, diag[:, :], ALU.add, ALU.mult))
            dve.wait_ge(off_ready, 1)
            nc.vector.tensor_copy(rows[:, :, 1], bank[6][:, 0:T])
            link(nc.vector.tensor_tensor(last[:, :], bank[6][:, 0:T], deg[:, :], ALU.add))
            link(nc.vector.tensor_scalar(bad[:, 2, :], last[:, :], float(E), None, ALU.is_gt))
            link(nc.vector.tensor_reduce(bad_col[:, :], bad[:, :, :].rearrange("p a t -> p (a t)"), AX.X, ALU.add))
            nc.vector.tensor_scalar(bad_col[:, :], bad_col[:, :], 1.0, None, ALU.min).then_inc(bad_rows, 1)
            dve.wait_ge(bad_sum, 1)
            nc.vector.tensor_scalar(bad_int[:, :], bank[6][0:1, 0:1], 1.0, None, ALU.min).then_inc(flag_ready, 1)
            link(nc.vector.scalar_tensor_tensor(minus_mid[:, :], deg[:, :], -0.5, rows[:, :, 1], ALU.mult, ALU.subtract))
            link(nc.vector.tensor_scalar(minus_mid[:, :], minus_mid[:, :], 0.5, None, ALU.add))
            nc.vector.scalar_tensor_tensor(reach[:, :], deg[:, :], 0.25, deg[:, :], ALU.mult, ALU.mult)\
              .then_inc(spans_ready, 1)
            dve.wait_ge(spans_ready, 1)

            def own_edges(t, j):
                dve.wait_ge(dist_ready, t + 1)
                nc.vector.tensor_scalar(row_to_edge[j], edge_dist, reach[:, bass.ds(t, 1)], None,
                                        ALU.is_lt).then_inc(rte_ready, 1)

            def list_edges(t, j):
                wait(dve, etr_ready, t - 1)
                dve.wait_ge(edge_rows_ready, t + 1)
                taken = bank[0][:, 0:C * NA].rearrange("p (c n) -> p c n", c=C)
                nc.vector.tensor_copy(edge_row[j % 2][:, :], taken[:, :, 0])
                link(nc.vector.tensor_tensor(slot[:, :], edge_no[:, :], taken[:, :, 1], ALU.subtract))
                link(nc.vector.tensor_tensor(slot_is[j][:, :, :], iota_s[:, :, :],
                                             slot[:, :].unsqueeze(2).to_broadcast([P, C, S]), ALU.is_equal))
                nc.vector.tensor_tensor(nb_sel[:, :, :], slot_is[j][:, :, :], taken[:, :, 2:NA], ALU.mult)\
                  .then_inc(edge_rows_read, 1)
                dve.wait_ge(edge_rows_read, t + 1)
                link(nc.vector.tensor_reduce(nb_f[:, :], nb_sel[:, :, :], AX.X, ALU.add))
                nc.vector.tensor_scalar(nb_idx[j % 2][:, :], nb_f[:, :], -1.0, float(LB + N - 1), ALU.mult,
                                        ALU.add).then_inc(nb_ready, 1)

            def own_row(t, j):
                nc.vector.tensor_tensor(edge_to_row[j % 2][:, :, :],
                                        edge_row[j % 2][:, :].unsqueeze(2).to_broadcast([P, C, P]),
                                        iota_q1[:, :].unsqueeze(1).to_broadcast([P, C, P]),
                                        ALU.is_equal).then_inc(etr_ready, 1)

            def multiply(t, j, n_in):
                dve.wait_ge(own_in[j], n_in)
                nc.vector.tensor_tensor(prod[:, C, :], q_sb[:, bass.ds(t, 1), :].rearrange("p o n -> p (o n)"),
                                        kv_e[j][:, C, 0:D], ALU.mult)
                for c in range(0, C, 2):
                    m = min(2, C - c)
                    dve.wait_ge(q_edges, t * 3 + (c // 2 + 1))
                    for i in range(m):
                        dve.wait_ge(nb_in[j][c + i], n_in)
                    nc.vector.tensor_tensor(prod[:, c:c + m, :],
                                            bank[2 + c // 2][:, 0:m * D].rearrange("p (c n) -> p c n", c=m),
                                            kv_e[j][:, c:c + m, 0:D], ALU.mult).then_inc(q_edges_read, 1)

            def scores(t):
                dve.wait_ge(q_edges_read, t * 3 + 3)
                link(nc.vector.tensor_reduce(score[:, :, :].rearrange("p c h -> p (c h)"),
                                             prod[:, :, :].rearrange("p c (h d) -> p (c h) d", d=DK), AX.X, ALU.add))
                nc.vector.tensor_copy(own[:, :], score[:, C, :]).then_inc(own_score, 1)

            def into_slots(t, j):
                dve.wait_ge(own_spread, t + 1)
                link(nc.vector.tensor_tensor(score_d[:, :, :], score[:, 0:C, :],
                                             bank[1][:, 0:C * H].rearrange("p (c h) -> p c h", c=C), ALU.subtract))
                nc.vector.tensor_tensor(spread[:, :, :, :], score_d[:, :, :].unsqueeze(2).to_broadcast([P, C, S, H]),
                                        slot_is[j][:, :, :].unsqueeze(3).to_broadcast([P, C, S, H]),
                                        ALU.mult).then_inc(slots_ready, 1)

            def maximum(t):
                dve.wait_ge(slots_filled, t + 1)
                link(nc.vector.tensor_reduce(top_raw[:, :], bank[1][:, 0:S * H].rearrange("p (s h) -> p h s", s=S),
                                             AX.X, ALU.max))
                nc.vector.tensor_scalar(top[:, :], top_raw[:, :], 0.0, None, ALU.max).then_inc(top_ready, 1)

            def below_maximum(t):
                dve.wait_ge(top_spread, t + 1)
                nc.vector.tensor_tensor(score_m[:, :, :], score_d[:, :, :],
                                        bank[1][:, 0:C * H].rearrange("p (c h) -> p c h", c=C),
                                        ALU.subtract).then_inc(shifted, 1)

            def weigh_values(t, j):
                dve.wait_ge(weights_ready, t + 1)
                nc.vector.tensor_tensor(pv[:, :, 0:D].rearrange("p c (h d) -> p c h d", h=H),
                                        kv_e[j][:, :, D:2 * D].rearrange("p c (h d) -> p c h d", h=H),
                                        pv[:, :, D:D + H].unsqueeze(3).to_broadcast([P, C + 1, H, DK]),
                                        ALU.mult).then_inc(pv_ready, 1)

            def normalise(t, j):
                dve.wait_ge(pv_ready, t + 1)
                dve.wait_ge(ctx_summed, t + 1)
                link(nc.vector.tensor_tensor(ctx_acc[:, :], bank[5][:, 0:D + H], pv[:, C, :], ALU.add))
                link(nc.vector.reciprocal(inv_den[:, :], ctx_acc[:, D:D + H]))
                nc.vector.tensor_tensor(att[:, j, :].rearrange("p (h d) -> p h d", h=H),
                                        ctx_acc[:, 0:D].rearrange("p (h d) -> p h d", h=H),
                                        inv_den[:, :].unsqueeze(2).to_broadcast([P, H, DK]),
                                        ALU.mult).then_inc(att_ready, 1)

            def moments(ln):
                link(nc.vector.bn_stats(stats[ln][:, :], h_sum[ln][:, :]), settled=True)
                link(nc.vector.bn_aggr(mean_var[ln][:, :], stats[ln][:, :]))
                nc.vector.tensor_scalar(mean_var[ln][:, 0:1], mean_var[ln][:, 0:1], -1.0, None, ALU.mult)
                nc.vector.tensor_scalar(mean_var[ln][:, 1:2], mean_var[ln][:, 1:2], EPS, None, ALU.add)\
                  .then_inc(var_ready[ln], 1)

            def first_sum(n, j):
                dve.wait_ge(x_bo_ready, n + 1)
                dve.wait_ge(proj_ready, n + 1)
                wait(dve, h1_ready, n)
                nc.vector.tensor_tensor(h_sum[0][:, :], bank[7][:, 0:D], x_res[j][:, :], ALU.add).then_inc(res_added, 1)
                settled_wait(dve, res_added, n + 1)
                moments(0)

            def second_sum(u, k):
                n = u * GT + k
                dve.wait_ge(h1_b2_ready, n + 1)
                dve.wait_ge(ff2_ready, n + 1)
                wait(dve, y_ready, n)
                nc.vector.tensor_tensor(h_sum[1][:, :], bank[6 + k % 2][:, 0:D], h1_b2[k], ALU.add).then_inc(ff2_read, 1)
                settled_wait(dve, ff2_read, n + 1)
                moments(1)

            def slot_work(turn, j):
                s = turn * GT + j
                if exists(s):
                    into_slots(s, j)
                if exists((turn - 2) * GT) and j < 2:
                    second_sum(turn - 2, 2 * j + 1)
                if exists(s + 2):
                    own_edges(s + 2, (j + 2) % GT)
                if exists(s + 1):
                    multiply(s + 1, (j + 1) % GT, (turn + (j + 1) // GT) * 16 + 16)
                if exists(s - 1):
                    first_sum(s - 1, (j - 1) % GT)
                if exists(s):
                    maximum(s)
                if exists(s + 1):
                    scores(s + 1)
                if exists(s):
                    below_maximum(s)
                if exists(s + 2):
                    list_edges(s + 2, (j + 2) % GT)
                if exists(s + 1):
                    own_row(s + 1, (j + 1) % GT)
                if exists((turn - 2) * GT) and j == 0:
                    second_sum(turn - 2, 2)
                if exists((turn - 1) * GT) and j == 3:
                    second_sum(turn - 1, 0)
                if exists(s):
                    weigh_values(s, j)
                    normalise(s, j)

            run_slots(dve, slot_work, steps)

            def dense():
                mask_steps, head_steps = counter(), counter()

                def mlink(ins):
                    ins.then_inc(mask_step, 1)
                    settled_wait(dve, mask_step, raised(mask_steps))

                def hlink(ins, settled=False):
                    ins.then_inc(dense_step, 1)
                    (settled_wait if settled else wait)(dve, dense_step, raised(head_steps))

                nc.vector.memset(top[:, 0:1], 0.0).then_inc(free_made, 1)
                nc.vector.memset(top[:, 1:2], 0.0).then_inc(kT_copied, 1)
                nc.vector.memset(top[:, 2:3], 0.0).then_inc(head_free, 1)
                with dve.Fori(0, T) as m:
                    dve.wait_ge(kT_ps, m + 1)
                    nc.vector.tensor_copy(d_kT_out, bank[0][:, 0:KD * P].rearrange("p (k n) -> p k n", k=KD))\
                        .then_inc(kT_copied, 1)
                with dve.Fori(0, G) as g:
                    with dve.Fori(0, GT) as j:
                        t = g * GT + j
                        enter(mask_steps, t, 0, 2)
                        dve.wait_ge(mask_in, t * 16 + 16)
                        mlink(nc.vector.scalar_tensor_tensor(d_junk[:, :], d_mask[:, bass.ds(t * P, P)], -1.0,
                                                             ident[:, :], ALU.mult, ALU.not_equal))
                        mlink(nc.vector.tensor_copy(d_mask[:, bass.ds(t * P, P)], d_junk[:, :]))
                        with dve.Fori(0, H) as h:
                            n = t * H + h
                            enter(head_steps, n, 0, 5)
                            nc.vector.tensor_copy(d_q, q_sb[:, bass.ds(t, 1), bass.ds(h * DK, DK)]
                                                  .rearrange("p o n -> p (o n)")).then_inc(head_q, 1)
                            dve.wait_ge(qT_ps, n + 1)
                            nc.vector.tensor_copy(d_qT, bank[0][0:DK, 0:P]).then_inc(qT_ready, 1)
                            hlink(nc.vector.memset(d_score, -1e9 / SCALE), settled=True)
                            for c in range(NS):
                                settled_wait(dve, scores_ps, n * NS + (c + 1))
                                nc.vector.copy_predicated(d_score[:, c * SC:(c + 1) * SC], d_mask[:, c * SC:(c + 1) * SC],
                                                          bank[2 + c % 2][:, :]).then_inc(scores_kept, 1)
                            dve.wait_ge(scores_kept, n * NS + NS)
                            hlink(nc.vector.tensor_reduce(d_max, d_score, AX.X, ALU.max))
                            nc.vector.tensor_scalar(d_shift, d_max, -SCALE, None, ALU.mult).then_inc(shift_ready, 1)
                            dve.wait_ge(head_summed, n + 1)
                            hlink(nc.vector.reciprocal(d_inv, d_den))
                            hlink(nc.vector.tensor_scalar(att[:, bass.ds(j, 1), bass.ds(h * DK, DK)]
                                                          .rearrange("p o n -> p (o n)"), bank[5][:, 0:DK], d_inv, None,
                                                          ALU.mult))
                            hlink(nc.vector.memset(d_max, 0.0))
                            nc.vector.memset(d_max, 0.0).then_inc(head_free, 1)
                        nc.vector.memset(inv_den[:, 4:5], 0.0).then_inc(att_ready, 1)
                        leave(mask_steps, 0)
                        leave(head_steps, 0)
                    u = g + G
                    enter(steps, g, 0, 2 * GT * LN_LINKS)
                    for k in range(GT):
                        first_sum(u * GT + k, k)
                    for k in range(GT):
                        second_sum(u, k)
                    leave(steps, G)

            if_dense(dve, dense)

        @block.tensor
        def _(pe):
            pe.wait_ge(qkv_in, QKV_IN)
            pe.wait_ge(consts_made, CONSTS)

            def pack_turn(i):
                for half in range(2):
                    for b in range(2):
                        t = i * GT + half * 2 + b
                        pe.wait_ge(xT_in[b], (i * 2 + half) * 16 + 16)
                        wait(pe, q_ready, t - 1)
                        for k in range(KD):
                            nc.tensor.matmul(bank[b][:, :], xT_sb[b][:, k, :], wkv_sb[:, k, :], start=k == 0, stop=k == KD - 1)
                        for k in range(KD):
                            ins = nc.tensor.matmul(bank[2 + b][:, 0:D], xT_sb[b][:, k, :], wq_sb[:, k, :],
                                                   start=k == 0, stop=k == KD - 1)
                        ins.then_inc(qkv_ready, 1)
                    for b in range(2):
                        t, j = i * GT + half * 2 + b, half * 2 + b
                        pe.wait_ge(diag_cleared, t + 1)
                        for a in range(A):
                            nc.tensor.matmul(bank[4 + j][:, 0:B], bit_diag[:, a, :],
                                             adj_b[b][:, (A - 1 - a) * B:(A - a) * B], start=a == 0, stop=False)
                        nc.tensor.matmul(bank[4 + j][:, 0:B], bit_diag[:, A, :], word_no[:, :],
                                         start=False, stop=True).then_inc(words_ready, 1)

            turns(pe, pack_turn, T // GT)

            pe.wait_ge(consts_in, CONSTS_IN)
            pe.wait_ge(deg_ready, 1)
            nc.tensor.matmul(bank[6][:, 0:T], before[:, :], deg[:, :], start=True, stop=True).then_inc(off_ready, 1)
            pe.wait_ge(bad_rows, 1)
            nc.tensor.matmul(bank[6][0:1, 0:1], bad_col[:, :], ones_col[:, :], start=True, stop=True).then_inc(bad_sum, 1)

            def to_edges(j, what, width, psum):
                for c in range(C):
                    ins = nc.tensor.matmul(psum[:, c * width:(c + 1) * width], row_to_edge[j][:, c * P:(c + 1) * P],
                                           what, start=True, stop=True)
                return ins

            def edges(t, j):
                pe.wait_ge(rte_ready, t + 1)
                wait(pe, edge_rows_read, t)
                to_edges(j, rows[:, bass.ds(t, 1), :].rearrange("p o n -> p (o n)"), NA,
                         bank[0]).then_inc(edge_rows_ready, 1)

            def queries(t, j):
                for c in range(C):
                    if c % 2 == 0:
                        wait(pe, q_edges_read, (t - 1) * 3 + (c // 2 + 1))
                    ins = nc.tensor.matmul(bank[2 + c // 2][:, c % 2 * D:c % 2 * D + D],
                                           row_to_edge[j][:, c * P:(c + 1) * P],
                                           q_sb[:, bass.ds(t, 1), :].rearrange("p o n -> p (o n)"), start=True, stop=True)
                    if c % 2 == 1 or c == C - 1:
                        ins.then_inc(q_edges, 1)

            def spread_own(t, j):
                wait(pe, shifted, t)
                pe.wait_ge(own_score, t + 1)
                to_edges(j, own[:, :], H, bank[1]).then_inc(own_spread, 1)

            def fill_slots(t, j):
                pe.wait_ge(slots_ready, t + 1)
                for c in range(C):
                    ins = nc.tensor.matmul(bank[1][:, 0:S * H], edge_to_row[j % 2][:, c, :],
                                           spread[:, c, :, :].rearrange("p s h -> p (s h)"), start=c == 0, stop=c == C - 1)
                ins.then_inc(slots_filled, 1)

            def spread_top(t, j):
                pe.wait_ge(top_ready, t + 1)
                to_edges(j, top[:, :], H, bank[1]).then_inc(top_spread, 1)

            def sum_values(t, j):
                pe.wait_ge(pv_ready, t + 1)
                wait(pe, att_ready, t)
                for c in range(C):
                    ins = nc.tensor.matmul(bank[5][:, 0:D + H], edge_to_row[j % 2][:, c, :], pv[:, c, :],
                                           start=c == 0, stop=c == C - 1)
                ins.then_inc(ctx_summed, 1)

            def turn_att(n, j):
                pe.wait_ge(att_ready, n + 1)
                for k in range(KD):
                    ins = nc.tensor.transpose(bank[6][:, k * P:(k + 1) * P], att[:, j, k * P:(k + 1) * P], ident[:, :])
                ins.then_inc(attT_ps, 1)

            def project(n):
                pe.wait_ge(attT_ready, n + 1)
                wait(pe, res_added, n)
                for k in range(KD):
                    ins = nc.tensor.matmul(bank[7][:, 0:D], attT[:, k, :], wo_sb[:, k, :], start=k == 0, stop=k == KD - 1)
                ins.then_inc(proj_ready, 1)

            def turn_h1(u, k):
                pe.wait_ge(h1_ready, u * GT + GT)
                for i in range(GT):
                    ins = nc.tensor.transpose(bank[6][:, i * P:(i + 1) * P], h1[i][:, k * P:(k + 1) * P], ident[:, :])
                ins.then_inc(h1T_ps, 1)

            def ff1(u, f):
                pe.wait_ge(h1T_ready, u * KD + KD)
                wait(pe, hidden_ready, u * KF + (f - 1))
                for k in range(KD):
                    ins = nc.tensor.matmul(bank[6 + f % 2][:, :], w1_sb[:, k, f * P:(f + 1) * P], h1T[:, k, :],
                                           start=k == 0, stop=k == KD - 1)
                ins.then_inc(ff1_ready, 1)

            def ff2(u, k):
                pe.wait_ge(hidden_ready, u * KF + KF)
                wait(pe, ff2_read, u * GT + (k - 1))
                for f in range(KF):
                    ins = nc.tensor.matmul(bank[6 + k % 2][:, 0:D], uT[:, f, k * P:(k + 1) * P], w2_sb[:, f, :],
                                           start=f == 0, stop=f == KF - 1)
                ins.then_inc(ff2_ready, 1)

            def slot(turn, j):
                s = turn * GT + j
                behind, before_it = exists((turn - 1) * GT), exists((turn - 2) * GT)
                if behind and j == 1:
                    pe.wait_ge(h1T_ready, (turn - 1) * KD + 1)
                    turn_h1(turn - 1, 1)
                if exists(s - 1):
                    wait(pe, *((ff2_read, (turn - 2) * GT + 1), (h1T_ready, (turn - 1) * KD + KD),
                               (hidden_ready, (turn - 1) * KF + 3), (hidden_ready, (turn - 1) * KF + 7))[j])
                    turn_att(s - 1, (j - 1) % GT)
                if exists(s):
                    fill_slots(s, j)
                if exists(s - 1):
                    wait(pe, *((ff2_read, (turn - 2) * GT + 2), (ff2_read, (turn - 2) * GT + 4),
                               (hidden_ready, (turn - 1) * KF + 4), (hidden_ready, (turn - 1) * KF + 8))[j])
                    project(s - 1)
                if before_it and j == 0:
                    ff2(turn - 2, 2)
                if behind and j in (1, 2):
                    ff1(turn - 1, 4 * (j - 1))
                if behind and j == 3:
                    ff2(turn - 1, 0)
                if exists(s):
                    spread_top(s, j)
                if exists(s + 2):
                    edges(s + 2, (j + 2) % GT)
                if exists(s + 1):
                    spread_own(s + 1, (j + 1) % GT)
                if exists(s + 2):
                    queries(s + 2, (j + 2) % GT)
                if exists(s):
                    sum_values(s, j)
                if behind or before_it:
                    if exists(s - 1):
                        pe.wait_ge(res_added, s)
                if before_it and j == 0:
                    ff2(turn - 2, 3)
                if behind and j in (1, 2):
                    if j == 1:
                        wait(pe, ff2_read, (turn - 2) * GT + 4)
                    for i in range(1, 4):
                        ff1(turn - 1, 4 * (j - 1) + i)
                if behind and j == 3:
                    ff2(turn - 1, 1)
                if behind and j == 0:
                    wait(pe, ff2_read, (turn - 2) * GT + 3)
                    turn_h1(turn - 1, 0)

            run_slots(pe, slot)

            def dense():
                with pe.Fori(0, T) as m:
                    pe.wait_ge(k_rows_in, m * 16 + 16)
                    for k in range(KD):
                        ins = nc.tensor.transpose(bank[0][:, k * P:(k + 1) * P], d_k_rows[:, k * P:(k + 1) * P], ident[:, :])
                    ins.then_inc(kT_ps, 1)
                with pe.Fori(0, G) as g:
                    with pe.Fori(0, GT) as j:
                        with pe.Fori(0, H) as h:
                            n = (g * GT + j) * H + h
                            pe.wait_ge(head_q, n + 1)
                            nc.tensor.transpose(bank[0][0:DK, 0:P], d_q, ident[:, :]).then_inc(qT_ps, 1)
                            pe.wait_ge(qT_ready, n + 1)
                            pe.wait_ge(head_in, n * 32 + 32)
                            for c in range(NS):
                                if c >= 2:
                                    pe.wait_ge(scores_kept, n * NS + (c - 1))
                                nc.tensor.matmul(bank[2 + c % 2][:, :], d_qT, d_kT[:, c * SC:(c + 1) * SC],
                                                 start=True, stop=True).then_inc(scores_ps, 1)
                            pe.wait_ge(probs_ready, n + 1)
                            for m in range(M4 + 1):
                                if m < M4:
                                    if m >= 2:
                                        pe.wait_ge(pT_ready, n * M4 + (m - 1))
                                    for i in range(4):
                                        ins = nc.tensor.transpose(bank[m % 2][:, i * P:(i + 1) * P],
                                                                  d_score[:, (m * 4 + i) * P:(m * 4 + i + 1) * P], ident[:, :])
                                    ins.then_inc(pT_ps, 1)
                                if m >= 1:
                                    pe.wait_ge(pT_ready, n * M4 + m)
                                    for i in range(4):
                                        c = (m - 1) * 4 + i
                                        ins = nc.tensor.matmul(bank[5][:, 0:DK], d_pT[(m - 1) % 2][:, i * P:(i + 1) * P],
                                                               d_v[:, c, :], start=c == 0, stop=c == T - 1)
                            ins.then_inc(head_summed, 1)
                    u = g + G
                    pe.wait_ge(ff2_read, u * GT)
                    for k in range(GT):
                        turn_att(u * GT + k, k)
                        project(u * GT + k)
                    pe.wait_ge(res_added, u * GT + GT)
                    for k in range(KD):
                        if k > 0:
                            pe.wait_ge(h1T_ready, u * KD + k)
                        turn_h1(u, k)
                    for f in range(KF):
                        ff1(u, f)
                    for k in range(GT):
                        ff2(u, k)

            if_dense(pe, dense)


def kernel(x, adj, L0_gnn_Wq, L0_gnn_bq, L0_gnn_Wk, L0_gnn_bk, L0_gnn_Wv, L0_gnn_bv, L0_gnn_Wo, L0_gnn_bo, L0_gnn_W1,
           L0_gnn_b1, L0_gnn_W2, L0_gnn_b2, L0_gnn_ln1_g, L0_gnn_ln1_b, L0_gnn_ln2_g, L0_gnn_ln2_b):
    import numpy as np
    import concourse.bacc as bacc
    from concourse.bass_utils import run_bass_kernel_spmd

    laid_out = {
        "x": x, "xT": np.asarray(x).T, "adj": adj, "wqT": np.asarray(L0_gnn_Wq).T, "wkT": np.asarray(L0_gnn_Wk).T,
        "wvT": np.asarray(L0_gnn_Wv).T, "woT": np.asarray(L0_gnn_Wo).T, "w1T": np.asarray(L0_gnn_W1).T,
        "w2T": np.asarray(L0_gnn_W2).T, "bq": L0_gnn_bq, "bk": L0_gnn_bk, "bv": L0_gnn_bv, "bo": L0_gnn_bo,
        "b1": L0_gnn_b1, "b2": L0_gnn_b2, "ln1_g": L0_gnn_ln1_g, "ln1_b": L0_gnn_ln1_b, "ln2_g": L0_gnn_ln2_g,
        "ln2_b": L0_gnn_ln2_b,
    }
    arrays = {f"in_{name}": np.ascontiguousarray(a) for name, a in laid_out.items()}
    nc = bacc.Bacc("TRN2", target_bir_lowering=False, num_devices=1)
    aps = [nc.dram_tensor(name, a.shape, mybir.dt.from_np(a.dtype), kind="ExternalInput").ap() for name, a in arrays.items()]
    out = nc.dram_tensor("out_h", arrays["in_x"].shape, mybir.dt.float32, kind="ExternalOutput").ap()
    graph_attention_kernel(nc, *aps, out)
    result = run_bass_kernel_spmd(nc, [arrays], core_ids=[0])
    return result.results[0]["out_h"]
```

```python
import concourse.bass as bass
from concourse import mybir
from contextlib import ExitStack


def graph_attention_kernel(nc, x, xT, adj, wqT, wkT, wvT, woT, w1T, w2T,
                           bq, bk, bv, bo, b1, b2, ln1_g, ln1_b, ln2_g, ln2_b, out):
    fp32, bf16, i32, u32 = mybir.dt.float32, mybir.dt.bfloat16, mybir.dt.int32, mybir.dt.uint32
    fp32r = mybir.dt.float32r
    ALU = mybir.AluOpType
    ACT = mybir.ActivationFunctionType
    AX = mybir.AxisListType

    N, D = x.shape
    F = w1T.shape[1]
    P = 128
    T = N // P
    H = 8
    DK = D // H
    KD = D // P
    KF = F // P
    GT = 4
    G = T // GT
    A = 16
    B = N // A
    S = 16
    R = 3
    C = 5
    E = C * P
    QB = 2 ** 8
    LB = (127 + 8) * B
    assert N <= 4096
    EXP_BITS = -(1 << 23)
    SCALE = float(DK) ** -0.5
    EPS = 1e-5
    PACK_LINKS = GT // 2 * 28
    LN_LINKS = 2
    SLOT_LINKS = 10
    TURN_LINKS = GT * (SLOT_LINKS + 2 * LN_LINKS)
    OWN = S + 2
    NA = OWN + 2 * H

    kv_dram = nc.dram_tensor("kv_scratch", [N, 2 * D], fp32, kind="Internal").ap()
    kT_dram = nc.dram_tensor("kT_scratch", [D, N], fp32, kind="Internal").ap()
    xT_v = xT.rearrange("(k p) n -> p k n", p=P)

    ctx = ExitStack()
    with ctx:
        def sb(name, shape, dt=fp32):
            return ctx.enter_context(nc.sbuf_tensor(name, shape, dt))

        def sem(name):
            return ctx.enter_context(nc.semaphore(name))

        bank = [ctx.enter_context(nc.psum_tensor(f"bank{i}", [P, 512], fp32)) for i in range(8)]

        wq_sb = sb("wq_sb", [P, KD, D])
        wkv_sb = sb("wkv_sb", [P, KD, 2 * D])
        wo_sb = sb("wo_sb", [P, KD, D])
        w1_sb = sb("w1_sb", [P, KD, F])
        w2_sb = sb("w2_sb", [P, KF, D])
        bq_sb = sb("bq_sb", [P, D])
        bkv_sb = sb("bkv_sb", [P, 2 * D])
        bo_sb = sb("bo_sb", [P, D])
        b2_sb = sb("b2_sb", [P, D])
        g1_sb = sb("g1_sb", [P, D])
        be1_sb = sb("be1_sb", [P, D])
        g2_sb = sb("g2_sb", [P, D])
        be2_sb = sb("be2_sb", [P, D])
        b1_sb = sb("b1_sb", [P, KF])
        ident = sb("ident", [P, P])
        off_diag = sb("off_diag", [P, P], bf16)
        before = sb("before", [P, P])
        ones_col = sb("ones_col", [P, 1])
        bit_diag = sb("bit_diag", [P, A + 1, P], bf16)
        word_no = sb("word_no", [P, B], bf16)
        iota_e = sb("iota_e", [P, E])
        edge_no = sb("edge_no", [P, C])
        iota_s = sb("iota_s", [P, C, S])
        iota_q1 = sb("iota_q1", [P, P])
        neg_half = sb("neg_half", [P, 1])
        CONSTS = (A + 3) + 3 + 6
        QKV_IN, CONSTS_IN = 6 * 16, 10 * 16

        q_sb = sb("q_sb", [P, T, D])
        rows = sb("rows", [P, T, NA], fp32r)
        row_no1 = sb("row_no1", [P, 1])
        deg = sb("deg", [P, T])
        last = sb("last", [P, T])
        minus_mid = sb("minus_mid", [P, T])
        reach = sb("reach", [P, T])
        row_sum = sb("row_sum", [P, T])
        diag = sb("diag", [P, T])
        bad = sb("bad", [P, 3, T])
        bad_col = sb("bad_col", [P, 1])
        bad_int = sb("bad_int", [1, 1], i32)

        adj_i_sb = sb("adj_i_sb", [P, 2, N], i32)
        adj_b_sb = sb("adj_b_sb", [P, 2, N], bf16)
        adj_i = [adj_i_sb[:, b, :] for b in range(2)]
        adj_b = [adj_b_sb[:, b, :] for b in range(2)]
        xT_sb = [sb(f"xT_sb{b}", [P, KD, P]) for b in range(2)]
        kv_out = [sb(f"kv_out{b}", [P, 2 * D]) for b in range(2)]
        diag_i = sb("diag_i", [P, T], i32)
        words = sb("words", [P, 2, S])
        words_left = [sb(f"words_left{b}", [P, B]) for b in range(2)]
        bits = sb("bits", [P, 2, R, S])
        rest = sb("rest", [P, R - 1, 2, S])
        words_i = sb("words_i", [P, 2, S], i32)
        word_at = sb("word_at", [P, 2, S], i32)
        codes = sb("codes", [P, 2, R, S], i32)
        found = sb("found", [P, 2, R, S])
        neighbours = sb("neighbours", [P, 2, S])
        found_left = sb("found_left", [P, 2, R * S])
        d_junk = sb("d_junk", [P, P])

        def region(first, words):
            return {"words": first, "at": 0, "size": words}

        def placed(where, name, words):
            at = where["at"]
            if at + words > where["size"]:
                return sb(name, [P, words])[:, :]
            where["at"] += words
            return where["words"][:, at:at + words]

        in_adj_b = region(adj_b_sb[:, :, :].rearrange("p b n -> p (b n)").bitcast(fp32), N)
        in_adj_i1 = region(adj_i[1].bitcast(fp32), N)
        in_xT = [region(xT_sb[b][:, :, :].rearrange("p k n -> p (k n)"), KD * P) for b in range(2)]
        in_kv_out = [region(kv_out[b][:, :], 2 * D) for b in range(2)]

        in_bit_diag = region(bit_diag[:, :, :].rearrange("p a n -> p (a n)")[:, 0:A * P].bitcast(fp32), A * P // 2)
        in_bkv = region(bkv_sb[:, :], 2 * D)
        in_wq = region(wq_sb[:, :, :].rearrange("p k n -> p (k n)"), KD * D)
        in_wkv = region(wkv_sb[:, :, :].rearrange("p k n -> p (k n)"), KD * 2 * D)

        edge_dist = placed(in_bit_diag, "edge_dist", E)
        KV = (C + 1) * 2 * D
        kv_e_sb = sb("kv_e_sb", [P, 2, C + 1, 2 * D])
        kv_e = [kv_e_sb[:, b, :, :] for b in range(2)] + [
            placed(where, name, KV).rearrange("p (c n) -> p c n", c=C + 1)
            for where, name in ((in_adj_b, "kv_e2"), (in_adj_i1, "kv_e3"))]
        row_to_edge = [sb(f"row_to_edge{j}", [P, E], fp32r)[:, :] for j in range(GT)]
        edge_to_row = [sb(f"edge_to_row{b}", [P, C, P]) for b in range(2)]
        minus_row = [sb(f"minus_row{b}", [P, C]) for b in range(2)]
        slot = sb("slot", [P, C])
        slot_is = [placed(in_adj_i1, f"slot_is{j}", C * S).rearrange("p (c s) -> p c s", c=C) for j in range(GT)]
        nb_sel = sb("nb_sel", [P, C, S])
        nb_f = sb("nb_f", [P, C])
        nb_idx = [sb(f"nb_idx{b}", [P, C], u32) for b in range(2)]
        prod = sb("prod", [P, C, D])
        score = sb("score", [P, C, H])
        score_d = sb("score_d", [P, C, H])
        spread = sb("spread", [P, C, S, H])
        own = sb("own", [P, 2, H])
        own_at_edge = [placed(in_adj_i1, f"own_at_edge{j}", C * H).rearrange("p (c h) -> p c h", c=C) for j in range(GT)]
        top_raw = sb("top_raw", [P, H])
        top = sb("top", [P, H])
        top_parts = sb("top_parts", [P, 2, H], fp32r)
        q_parts = sb("q_parts", [P, 2, D], fp32r)
        score_m = sb("score_m", [P, C, H])
        pv = sb("pv", [P, C + 1, D + H])
        ctx_acc = sb("ctx_acc", [P, D + H])
        inv_den = sb("inv_den", [P, H])

        att = sb("att", [P, GT, D])
        x_res = [placed(in_wkv, f"x_res{j}", D) for j in range(GT)]
        attT = placed(in_bit_diag, "attT", KD * P).rearrange("p (k n) -> p k n", k=KD)
        h_sum1 = sb("h_sum1", [P, D])[:, :]
        stats = [sb(f"stats{n}", [P, 6]) for n in range(2)]
        mean_var = [sb(f"mean_var{n}", [P, 2]) for n in range(2)]
        rstd = [sb(f"rstd{n}", [P, 1]) for n in range(2)]
        shift = [sb(f"shift{n}", [P, 1]) for n in range(2)]
        h1 = [placed(in_wq, f"h1_{j}", D) for j in range(GT)]
        h1_b2 = [placed(in_xT[j] if j < 2 else in_bkv, f"h1_b2_{j}", D) for j in range(GT)]
        h1T = placed(in_adj_b, "h1T", KD * GT * P).rearrange("p (k n) -> p k n", k=KD)
        HW = KF * GT * P
        hidden = adj_i_sb if 2 * N >= HW else sb("hidden", [P, 1, HW], i32)
        uT = hidden[:, :, :].rearrange("p b n -> p (b n)")[:, 0:HW].bitcast(fp32).rearrange("p (f n) -> p f n", f=KF)
        y = [placed(in_kv_out[j // 2], f"y{j}", D) for j in range(GT)]

        qkv_in = sem("qkv_in")
        consts_in = sem("consts_in")
        diag_in = sem("diag_in")
        ident_made = sem("ident_made")
        consts_made = sem("consts_made")
        adj_in = [sem(f"adj_in{b}") for b in range(2)]
        xT_in = [sem(f"xT_in{b}") for b in range(2)]
        qkv_ready = sem("qkv_ready")
        kv_ready = sem("kv_ready")
        q_ready = sem("q_ready")
        kv_stored = [sem(f"kv_stored{b}") for b in range(2)]
        adj_cast = sem("adj_cast")
        diag_cleared = sem("diag_cleared")
        words_ready = sem("words_ready")
        list_ready = sem("list_ready")
        dve_step = sem("dve_step")
        off_ready = sem("off_ready")
        bad_sum = sem("bad_sum")
        bad_rows = sem("bad_rows")
        deg_ready = sem("deg_ready")
        kv_cleared = sem("kv_cleared")
        flag_ready = sem("flag_ready")
        spans_ready = sem("spans_ready")
        dist_ready = sem("dist_ready")
        rte_ready = sem("rte_ready")
        edge_rows_ready = sem("edge_rows_ready")
        edge_rows_read = sem("edge_rows_read")
        nb_ready = sem("nb_ready")
        etr_squared = sem("etr_squared")
        etr_ready = sem("etr_ready")
        nb_in = [[sem(f"nb_in{j}_{c}") for c in range(C)] for j in range(GT)]
        own_in = [sem(f"own_in{j}") for j in range(GT)]
        q_rounded = sem("q_rounded")
        q_split = sem("q_split")
        q_edges = sem("q_edges")
        q_edges_read = sem("q_edges_read")
        slots_ready = sem("slots_ready")
        slots_filled = sem("slots_filled")
        top_ready = sem("top_ready")
        top_spread = sem("top_spread")
        shifted = sem("shifted")
        weights_ready = sem("weights_ready")
        pv_ready = sem("pv_ready")
        ctx_summed = sem("ctx_summed")
        att_ready = sem("att_ready")
        x_in = [sem(f"x_in{j}") for j in range(GT)]
        attT_ps = sem("attT_ps")
        attT_ready = sem("attT_ready")
        proj_ready = sem("proj_ready")
        x_bo_ready = sem("x_bo_ready")
        res_added = sem("res_added")
        var_ready = [sem(f"var{n}_ready") for n in range(2)]
        rstd_made = [sem(f"rstd{n}_made") for n in range(2)]
        rstd_ready = [sem(f"rstd{n}_ready") for n in range(2)]
        normed = [sem(f"normed{n}") for n in range(2)]
        gained = [sem(f"gained{n}") for n in range(2)]
        h1_ready = sem("h1_ready")
        h1_b2_ready = sem("h1_b2_ready")
        h1T_ps = sem("h1T_ps")
        h1T_ready = sem("h1T_ready")
        ff1_ready = sem("ff1_ready")
        hidden_ready = sem("hidden_ready")
        ff2_ready = sem("ff2_ready")
        ff2_read = sem("ff2_read")
        y_ready = sem("y_ready")
        y_out = [sem(f"y_out{j}") for j in range(GT)]
        free_made = sem("free_made")
        k_rows_in = sem("k_rows_in")
        kT_ps = sem("kT_ps")
        kT_copied = sem("kT_copied")
        kT_stored = sem("kT_stored")
        mask_in = sem("mask_in")
        mask_ready = sem("mask_ready")
        head_free = sem("head_free")
        head_in = sem("head_in")
        head_q = sem("head_q")
        qT_ps = sem("qT_ps")
        qT_ready = sem("qT_ready")
        scores_ps = sem("scores_ps")
        scores_kept = sem("scores_kept")
        shift_ready = sem("shift_ready")
        probs_ready = sem("probs_ready")
        pT_ps = sem("pT_ps")
        pT_ready = sem("pT_ready")
        head_summed = sem("head_summed")
        dense_step = sem("dense_step")
        mask_step = sem("mask_step")

        SC = 512
        NS = N // SC
        M4 = T // 4
        d_mask = adj_i[1]
        d_score = adj_b_sb[:, :, :].rearrange("p b n -> p (b n)").bitcast(fp32)
        kv_flat = kv_e_sb[:, :, :, :].rearrange("p b c n -> p (b c n)")
        d_k_rows = kv_flat[:, 0:D]
        d_kT_out = kv_flat[:, D:D + KD * P].rearrange("p (k n) -> p k n", k=KD)
        d_kT = kv_flat[0:DK, 0:N]
        d_v = prod[:, :, :].rearrange("p c n -> p (c n)")[:, 0:T * DK].rearrange("p (c d) -> p c d", c=T)
        pv_flat = pv[:, :, :].rearrange("p c n -> p (c n)")
        d_pT = [pv_flat[:, b * 512:(b + 1) * 512] for b in range(2)]
        d_q = ctx_acc[:, 0:DK]
        d_qT = spread[0:DK, 0, :, :].rearrange("p s h -> p (s h)")
        d_den, d_max, d_shift, d_inv = (inv_den[:, c:c + 1] for c in range(4))

        block = ctx.enter_context(nc.Block())

        def wait(eng, signal, value):
            if not isinstance(value, int) or value > 0:
                eng.wait_ge(signal, value)

        def settled_wait(eng, signal, value):
            if isinstance(value, int):
                wait(eng, signal, value)
                return
            with eng.register() as count:
                eng.reg_mov(count, value)
                eng.wait_ge(consts_made, CONSTS)
                eng.wait_ge(signal, count)

        def counter():
            return {"done": 0, "turn": None, "first": 0, "per_turn": 0, "here": 0}

        def enter(count, turn, first, per_turn):
            count["turn"], count["first"], count["per_turn"], count["here"] = turn, first, per_turn, 0

        def leave(count, turns):
            assert count["here"] == count["per_turn"], count["here"]
            count["done"] += turns * count["per_turn"]
            count["turn"] = None

        def raised(count):
            if count["turn"] is None:
                count["done"] += 1
                return count["done"]
            count["here"] += 1
            return (count["turn"] - count["first"]) * count["per_turn"] + (count["done"] + count["here"])

        def turns(eng, body, count, *chains):
            body(0)
            with eng.Fori(1, count - 1) as turn:
                for c in chains:
                    enter(c, turn, 1, PACK_LINKS)
                body(turn)
            for c in chains:
                leave(c, count - 2)
            body(count - 1)

        def exists(t):
            return not isinstance(t, int) or 0 <= t < T

        def run_slots(eng, slot, *chains):
            for j in range(GT - 2, GT):
                slot(-1, j)
            for turn in range(2):
                for j in range(GT):
                    slot(turn, j)
            if G > 3:
                with eng.Fori(2, G - 1) as turn:
                    for c in chains:
                        enter(c, turn, 2, TURN_LINKS)
                    for j in range(GT):
                        slot(turn, j)
                for c in chains:
                    leave(c, G - 3)
            for turn in range(G - 1, G + 1):
                for j in range(GT):
                    slot(turn, j)
            for j in range(GT):
                slot(G + 1, j)

        def if_dense(eng, run):
            eng.wait_ge(flag_ready, 1)
            flag = eng.value_load(bad_int[0:1, 0:1], min_val=0, max_val=1)
            with eng.If(flag > 0):
                run()

        @block.sync
        def _(sp):
            def tile_in(t, b):
                sp.dma_start(adj_i[b], adj[bass.ds(t * P, P), :]).then_inc(adj_in[b], 16)

            def input_in(t, b):
                sp.dma_start(xT_sb[b][:, :, :], xT_v[:, :, bass.ds(t * P, P)]).then_inc(xT_in[b], 16)

            def weights_in(signal, *pairs):
                for dst, w in pairs:
                    sp.dma_start(dst, w.rearrange("(k p) n -> p k n", p=P)).then_inc(signal, 16)

            def vectors_in(signal, *pairs):
                for dst, v in pairs:
                    sp.dma_start(dst, v.partition_broadcast(P)).then_inc(signal, 16)

            tile_in(0, 0)
            weights_in(qkv_in, (wkv_sb[:, :, 0:D], wkT), (wkv_sb[:, :, D:2 * D], wvT), (wq_sb[:, :, :], wqT))
            vectors_in(qkv_in, (bq_sb[:, :], bq), (bkv_sb[:, 0:D], bk), (bkv_sb[:, D:2 * D], bv))
            input_in(0, 0)
            tile_in(1, 1)
            input_in(1, 1)
            with nc.allow_non_contiguous_dma(reason="the diagonal's four thousand words, once"):
                sp.dma_start(diag_i[:, :], adj.rearrange("r c -> (r c)")[0:N * N:N + 1].rearrange("(t p) -> p t", p=P))\
                  .then_inc(diag_in, 16)

            def pack_turn(i):
                for j in range(GT):
                    t, b = i * GT + j, j % 2
                    if not (isinstance(t, int) and t + 2 >= T):
                        settled_wait(sp, adj_cast, t + 1)
                        tile_in(t + 2, b)
                        settled_wait(sp, qkv_ready, t + 1)
                        input_in(t + 2, b)
                    settled_wait(sp, kv_ready, t + 1)
                    sp.dma_start(kv_dram[bass.ds(t * P, P), :], kv_out[b][:, :]).then_inc(kv_stored[b], 16)

            turns(sp, pack_turn, T // GT)

            weights_in(consts_in, (wo_sb[:, :, :], woT), (w1_sb[:, :, :], w1T), (w2_sb[:, :, :], w2T))
            vectors_in(consts_in, (bo_sb[:, :], bo), (b2_sb[:, :], b2), (g1_sb[:, :], ln1_g), (be1_sb[:, :], ln1_b),
                       (g2_sb[:, :], ln2_g), (be2_sb[:, :], ln2_b))
            with nc.allow_non_contiguous_dma(reason="a thousand words, once"):
                sp.dma_start(b1_sb[:, :], b1.rearrange("(k p) -> p k", p=P)).then_inc(consts_in, 16)
            for b in range(2):
                sp.wait_ge(kv_stored[b], 16 * (T // 2))
            sp.wait_ge(kv_cleared, 3)

            def own_rows(t, j):
                settled_wait(sp, pv_ready, t - 3)
                sp.dma_start(kv_e[j][:, C, D:2 * D], kv_dram[bass.ds(t * P, P), D:2 * D]).then_inc(own_in[j], 16)

            def residual(n, j, row0):
                settled_wait(sp, res_added, n - 3)
                sp.dma_start(x_res[j], x[bass.ds(row0, P), :]).then_inc(x_in[j], 16)

            def store(u, k, row0):
                settled_wait(sp, y_ready, u * GT + (k + 1))
                sp.dma_start(out[bass.ds(row0, P), :], y[k]).then_inc(y_out[k], 16)

            own_rows(0, 0)

            def slot(turn, j):
                s = turn * GT + j
                if exists(s + 3):
                    own_rows(s + 3, (j + 3) % GT)
                if exists(s):
                    residual(s, j, s * P)
                if exists((turn - 2) * GT):
                    for k in ((), (), (0, 1), (2, 3))[j]:
                        store(turn - 2, k, (turn - 2) * (GT * P) + k * P)

            run_slots(sp, slot)

            def dense():
                settled_wait(sp, free_made, 1)
                with sp.Fori(0, T) as m:
                    settled_wait(sp, kT_copied, m + 1)
                    sp.dma_start(d_k_rows, kv_dram[bass.ds(m * P, P), 0:D]).then_inc(k_rows_in, 16)
                    settled_wait(sp, kT_copied, m + 2)
                    sp.dma_start(kT_dram.rearrange("(k p) n -> p k n", p=P)[:, :, bass.ds(m * P, P)],
                                 d_kT_out).then_inc(kT_stored, 16)
                    settled_wait(sp, kT_stored, m * 16 + 16)
                with sp.Fori(0, G) as g:
                    for k in range(GT):
                        residual((g + G) * GT + k, k, g * (GT * P) + k * P)
                    with sp.Fori(0, GT) as j:
                        settled_wait(sp, head_free, (g * GT + j) * H + 1)
                        sp.dma_start(d_mask, adj[bass.ds((g * GT + j) * P, P), :]).then_inc(mask_in, 16)
                        with sp.Fori(0, H) as h:
                            settled_wait(sp, head_free, (g * GT + j) * H + h + 1)
                            sp.dma_start(d_kT, kT_dram[bass.ds(h * DK, DK), :]).then_inc(head_in, 16)
                            sp.dma_start(d_v, kv_dram[:, bass.ds(h * DK + D, DK)].rearrange("(c p) d -> p c d", p=P))\
                              .then_inc(head_in, 16)
                    for k in range(GT):
                        store(g + G, k, g * (GT * P) + k * P)
                for k in range(GT):
                    sp.wait_ge(y_out[k], 32 * G)

            if_dense(sp, dense)
            for k in range(GT):
                sp.wait_ge(y_out[k], 16 * G)

        @block.gpsimd
        def _(pool):
            filled = [0]

            def diagonal(m, off, on):
                nc.gpsimd.memset(m, off).then_inc(ident_made, 1)
                filled[0] += 1
                pool.wait_ge(ident_made, filled[0])
                return nc.gpsimd.affine_select(out=m, in_=m, compare_op=ALU.not_equal, fill=on, base=0,
                                               pattern=[[-1, P]], channel_multiplier=1)
            for a in range(A):
                diagonal(bit_diag[:, a, :], 0.0, float(QB * 2 ** a)).then_inc(consts_made, 1)
            diagonal(bit_diag[:, A, :], 0.0, 1.0).then_inc(consts_made, 1)
            diagonal(off_diag[:, :], 1.0, 0.0).then_inc(consts_made, 1)
            diagonal(ident[:, :], 0.0, 1.0).then_inc(consts_made, 1)
            nc.gpsimd.memset(before[:, :], 1.0).then_inc(ident_made, 1)
            pool.wait_ge(ident_made, filled[0] + 1)
            nc.gpsimd.affine_select(out=before[:, :], in_=before[:, :], compare_op=ALU.is_gt, fill=0.0, base=0,
                                    pattern=[[1, P]], channel_multiplier=-1).then_inc(consts_made, 1)
            nc.gpsimd.memset(ones_col[:, :], 1.0).then_inc(consts_made, 1)
            nc.gpsimd.memset(neg_half[:, :], -0.5).then_inc(consts_made, 1)
            for m, pattern, base, per_partition in ((word_no[:, :], [[-1, B]], B - 1, 0), (iota_e[:, :], [[1, E]], 0, 0),
                                                    (edge_no[:, :], [[P, C]], 0, 1), (iota_s[:, :, :], [[0, C], [1, S]], 0, 0),
                                                    (iota_q1[:, :], [[1, P]], 1, 0), (row_no1[:, :], [[0, 1]], 1, 1)):
                nc.gpsimd.iota(m, pattern, base=base, channel_multiplier=per_partition,
                               allow_small_or_imprecise_dtypes=True).then_inc(consts_made, 1)
            nc.gpsimd.memset(kv_e_sb[:, :, :, :], 0.0).then_inc(kv_cleared, 1)
            pool.wait_ge(words_ready, T)
            pool.wait_ge(diag_cleared, T)
            for j in (2, 3):
                nc.gpsimd.memset(kv_e[j], 0.0).then_inc(kv_cleared, 1)
            pool.wait_ge(kv_cleared, 3)
            for b in range(2):
                pool.wait_ge(kv_stored[b], 16 * (T // 2))

            def gather(t, j):
                settled_wait(pool, nb_ready, t + 1)
                settled_wait(pool, pv_ready, t - 3)
                for c in range(C):
                    pool.indirect_dma_start(kv_e[j][:, c, :], None, kv_dram,
                                            bass.IndirectOffsetOnAxis(nb_idx[j % 2][:, c:c + 1], 0),
                                            bounds_check=N - 1, oob_is_err=False).then_inc(nb_in[j][c], 16)

            def inverse_root(ln, n):
                pool.wait_ge(var_ready[ln], n + 1)
                nc.gpsimd.tensor_tensor(rstd[ln][:, :], mean_var[ln][:, 1:2], neg_half[:, :], ALU.pow)\
                  .then_inc(rstd_made[ln], 1)
                pool.wait_ge(rstd_made[ln], n + 1)
                nc.gpsimd.tensor_tensor(shift[ln][:, :], mean_var[ln][:, 0:1], rstd[ln][:, :], ALU.mult)\
                  .then_inc(rstd_ready[ln], 1)

            def gain_shift(ln, n, h_sum, gain, bias, dst):
                pool.wait_ge(normed[ln], n + 1)
                nc.gpsimd.tensor_tensor(h_sum, h_sum, gain[:, :], ALU.mult).then_inc(gained[ln], 1)
                pool.wait_ge(gained[ln], n + 1)
                return nc.gpsimd.tensor_tensor(dst, h_sum, bias[:, :], ALU.add)

            def split_query(t):
                settled_wait(pool, q_rounded, t + 1)
                nc.gpsimd.tensor_tensor(q_parts[:, 1, :], q_sb[:, bass.ds(t, 1), :].rearrange("p o n -> p (o n)"),
                                        q_parts[:, 0, :].bitcast(fp32), ALU.subtract).then_inc(q_split, 1)

            def residual_bias(n, turn, j):
                pool.wait_ge(x_in[j], turn * 16 + 16)
                nc.gpsimd.tensor_tensor(x_res[j], x_res[j], bo_sb[:, :], ALU.add).then_inc(x_bo_ready, 1)

            def second_norm(u, k):
                gain_shift(1, u * GT + k, y[k], g2_sb, be2_sb, y[k]).then_inc(y_ready, 1)

            def slot(turn, j):
                s = turn * GT + j
                if exists(s + 1):
                    split_query(s + 1)
                if isinstance(turn, int) and s == 1:
                    pool.wait_ge(consts_in, CONSTS_IN)
                if exists(s - 1):
                    residual_bias(s - 1, turn - (j == 0), (j - 1) % GT)
                if exists((turn - 2) * GT) and j in (1, 2):
                    inverse_root(1, (turn - 2) * GT + (2 * j - 2))
                    second_norm(turn - 2, 2 * j - 2)
                if exists(s - 2):
                    inverse_root(0, s - 2)
                    wait(pool, h1T_ps, (turn - (j < 2)) * KD)
                    wait(pool, h1_b2_ready, s - 5)
                    gain_shift(0, s - 2, h_sum1, g1_sb, be1_sb, h1[(j - 2) % GT]).then_inc(h1_ready, 1)
                if exists((turn - 2) * GT) and j in (1, 2):
                    inverse_root(1, (turn - 2) * GT + (2 * j - 1))
                if exists(s + 2):
                    gather(s + 2, (j + 2) % GT)
                if exists((turn - 2) * GT) and j in (1, 2):
                    second_norm(turn - 2, 2 * j - 1)

            run_slots(pool, slot)

            def dense():
                with pool.Fori(0, G) as g:
                    u = g + G
                    for k in range(GT):
                        n = u * GT + k
                        residual_bias(n, u, k)
                        inverse_root(0, n)
                        gain_shift(0, n, h_sum1, g1_sb, be1_sb, h1[k]).then_inc(h1_ready, 1)
                    for k in range(GT):
                        inverse_root(1, u * GT + k)
                        second_norm(u, k)

            if_dense(pool, dense)

        @block.scalar
        def _(act):
            def pack_turn(i):
                for j in range(GT):
                    t, b = i * GT + j, j % 2
                    act.wait_ge(adj_in[b], (i * 2 + j // 2) * 16 + 16)
                    wait(act, words_ready, t - 1)
                    nc.scalar.activation(adj_b[b], adj_i[b], ACT.Square,
                                         accum_out=row_sum[:, bass.ds(t, 1)]).then_inc(adj_cast, 1)

            turns(act, pack_turn, T // GT)

            def weigh(t):
                act.wait_ge(shifted, t + 1)
                wait(act, ctx_summed, t)
                nc.scalar.activation(pv[:, 0:C, D:D + H], score_m[:, :, :], ACT.Exp, scale=SCALE)
                nc.scalar.activation(pv[:, C, D:D + H], top[:, :], ACT.Exp, scale=-SCALE).then_inc(weights_ready, 1)

            def distance(t):
                settled_wait(act, spans_ready, 1)
                settled_wait(act, rte_ready, t)
                nc.scalar.activation(edge_dist, iota_e[:, :], ACT.Square,
                                     bias=minus_mid[:, bass.ds(t, 1)]).then_inc(dist_ready, 1)

            def own_row(t, j):
                act.wait_ge(nb_ready, t + 1)
                wait(act, ctx_summed, t - 1)
                for c in range(C):
                    ins = nc.scalar.activation(edge_to_row[j % 2][:, c, :], iota_q1[:, :], ACT.Square,
                                               bias=minus_row[j % 2][:, c:c + 1])
                ins.then_inc(etr_squared, 1)
                act.wait_ge(etr_squared, t + 1)
                nc.scalar.activation(edge_to_row[j % 2][:, :, :], edge_to_row[j % 2][:, :, :], ACT.Relu, bias=1.0,
                                     scale=-1.0).then_inc(etr_ready, 1)

            def round_query(t):
                settled_wait(act, q_edges, t * 3)
                nc.scalar.activation(q_parts[:, 0, :], q_sb[:, bass.ds(t, 1), :].rearrange("p o n -> p (o n)"),
                                     ACT.Copy).then_inc(q_rounded, 1)

            def copy_att(n):
                act.wait_ge(attT_ps, n + 1)
                nc.scalar.activation(attT[:, :, :].rearrange("p k n -> p (k n)"), bank[6][:, 0:KD * P],
                                     ACT.Copy).then_inc(attT_ready, 1)

            def norm(ln, n, k):
                act.wait_ge(rstd_ready[ln], n + 1)
                h_sum = (h_sum1, y[k])[ln]
                nc.scalar.activation(h_sum, h_sum, ACT.Identity, bias=shift[ln][:, :],
                                     scale=rstd[ln][:, :]).then_inc(normed[ln], 1)

            def copy_h1(u, k):
                act.wait_ge(h1T_ps, u * KD + (k + 1))
                nc.scalar.activation(h1T[:, k, :], bank[7][:, :], ACT.Copy).then_inc(h1T_ready, 1)

            def relu(u, f):
                act.wait_ge(ff1_ready, u * KF + (f + 1))
                nc.scalar.activation(uT[:, f, :], bank[7 - f % 2][:, :], ACT.Relu,
                                     bias=b1_sb[:, f:f + 1]).then_inc(hidden_ready, 1)

            distance(0)

            def slot(turn, j):
                s = turn * GT + j
                if exists(s + 1):
                    round_query(s + 1)
                if exists((turn - 1) * GT) and j == 2:
                    copy_h1(turn - 1, 0)
                    copy_h1(turn - 1, 1)
                if exists((turn - 1) * GT) and j == 3:
                    relu(turn - 1, 2)
                if exists((turn - 2) * GT) and j == 0:
                    relu(turn - 2, 6)
                    relu(turn - 2, 7)
                if exists(s - 2):
                    copy_att(s - 2)
                if exists((turn - 2) * GT) and j in (1, 2):
                    norm(1, (turn - 2) * GT + (2 * j - 2), 2 * j - 2)
                if exists(s + 1):
                    own_row(s + 1, (j + 1) % GT)
                if exists(s + 3):
                    distance(s + 3)
                if exists(s - 2):
                    norm(0, s - 2, 0)
                if exists((turn - 1) * GT) and j >= 2:
                    relu(turn - 1, 3 * j - 6)
                if exists(s):
                    weigh(s)
                if exists((turn - 1) * GT) and j == 2:
                    relu(turn - 1, 1)
                if exists((turn - 1) * GT) and j == 3:
                    relu(turn - 1, 4)
                    relu(turn - 1, 5)
                if exists((turn - 2) * GT) and j in (1, 2):
                    norm(1, (turn - 2) * GT + (2 * j - 1), 2 * j - 1)

            run_slots(act, slot)

            def dense():
                with act.Fori(0, G) as g:
                    with act.Fori(0, GT) as j:
                        with act.Fori(0, H) as h:
                            n = (g * GT + j) * H + h
                            act.wait_ge(shift_ready, n + 1)
                            nc.scalar.activation(d_score, d_score, ACT.Exp, bias=d_shift, scale=SCALE,
                                                 accum_out=d_den).then_inc(probs_ready, 1)
                            for m in range(M4):
                                act.wait_ge(pT_ps, n * M4 + (m + 1))
                                nc.scalar.activation(d_pT[m % 2], bank[m % 2][:, :], ACT.Copy).then_inc(pT_ready, 1)
                    u = g + G
                    for k in range(GT):
                        copy_att(u * GT + k)
                        norm(0, u * GT + k, k)
                    for k in range(KD):
                        copy_h1(u, k)
                    for f in range(KF):
                        relu(u, f)
                    for k in range(GT):
                        norm(1, u * GT + k, k)

            if_dense(act, dense)

        @block.vector
        def _(dve):
            steps = counter()

            def link(ins, settled=False):
                ins.then_inc(dve_step, 1)
                (settled_wait if settled else wait)(dve, dve_step, raised(steps))

            def mark(ins):
                ins.then_inc(dve_step, 1)
                return raised(steps)

            def after(value, settled=False):
                (settled_wait if settled else wait)(dve, dve_step, value)

            dve.wait_ge(qkv_in, QKV_IN)
            dve.wait_ge(consts_made, CONSTS)

            def pack(t, b, stored):
                dve.wait_ge(qkv_ready, t + 1)
                wait(dve, kv_stored[b], stored)
                nc.vector.tensor_tensor(kv_out[b][:, :], bank[b][:, :], bkv_sb[:, :], ALU.add).then_inc(kv_ready, 1)
                nc.vector.tensor_tensor(q_sb[:, bass.ds(t, 1), :].rearrange("p o n -> p (o n)"), bank[2 + b][:, 0:D],
                                        bq_sb[:, :], ALU.add).then_inc(q_ready, 1)
                settled_wait(dve, q_ready, t + 1)
                product = mark(nc.vector.tensor_tensor(prod[:, b, :], q_sb[:, bass.ds(t, 1), :].rearrange("p o n -> p (o n)"),
                                                       kv_out[b][:, 0:D], ALU.mult))
                dve.wait_ge(adj_cast, t + 1)
                nc.vector.tensor_tensor(adj_b[b][:, bass.ds(t * P, P)], adj_b[b][:, bass.ds(t * P, P)], off_diag[:, :],
                                        ALU.mult).then_inc(diag_cleared, 1)
                after(product)
                return mark(nc.vector.tensor_reduce(own[:, b, :], prod[:, b, :].rearrange("p (h d) -> p h d", h=H),
                                                    AX.X, ALU.add))

            def own_parts(t):
                parts = [rows[:, bass.ds(t, 2), OWN + i * H:OWN + (i + 1) * H] for i in range(2)]
                rounded = mark(nc.vector.tensor_copy(parts[0], own[:, :, :]))
                after(rounded, settled=True)
                nc.vector.tensor_tensor(parts[1], own[:, :, :], parts[0].bitcast(fp32), ALU.subtract)

            def list_rows(t, j):
                settled_wait(dve, words_ready, t + 2)
                packed = [bank[4 + j + i][:, 0:B] for i in range(2)]
                for i in range(2):
                    link(nc.vector.max(words[:, i, 0:8], packed[i]), settled=True)
                for i in range(2):
                    link(nc.vector.match_replace(out=words_left[i][:, :], in_to_replace=words[:, i, 0:8],
                                                 in_values=packed[i], imm_value=0.0), settled=True)
                for i in range(2):
                    link(nc.vector.max(words[:, i, 8:16], words_left[i][:, :]), settled=True)
                left = words[:, :, :]
                for r in range(R):
                    link(nc.vector.tensor_scalar(bits[:, :, r, :].bitcast(i32), left.bitcast(i32), EXP_BITS, None,
                                                 ALU.bitwise_and))
                    if r < R - 1:
                        link(nc.vector.tensor_tensor(rest[:, r, :, :], left, bits[:, :, r, :], ALU.subtract))
                        left = rest[:, r, :, :]
                link(nc.vector.tensor_copy(words_i[:, :, :], words[:, :, :]))
                link(nc.vector.tensor_scalar(word_at[:, :, :], words_i[:, :, :], QB - 1, None, ALU.bitwise_and))
                link(nc.vector.tensor_scalar(codes[:, :, :, :], bits[:, :, :, :].bitcast(i32), 23, None,
                                             ALU.arith_shift_right))
                for i in range(2):
                    link(nc.vector.scalar_tensor_tensor(found[:, i, :, :], codes[:, i, :, :], float(B),
                                                        word_at[:, i, :].unsqueeze(1).to_broadcast([P, R, S]),
                                                        ALU.mult, ALU.add), settled=True)
                candidates = [found[:, i, :, :].rearrange("p r s -> p (r s)") for i in range(2)]
                for i in range(2):
                    link(nc.vector.max(neighbours[:, i, 0:8], candidates[i]), settled=True)
                for i in range(2):
                    link(nc.vector.match_replace(out=found_left[:, i, :], in_to_replace=neighbours[:, i, 0:8],
                                                 in_values=candidates[i], imm_value=0.0), settled=True)
                for i in range(2):
                    link(nc.vector.max(neighbours[:, i, 8:16], found_left[:, i, :]), settled=True)
                link(nc.vector.tensor_scalar(rows[:, bass.ds(t, 2), 2:OWN], neighbours[:, :, :], float(1 - LB), 0.0,
                                             ALU.add, ALU.max), settled=True)

            def pack_turn(i):
                for j in range(0, GT, 2):
                    t = i * GT + j
                    for b in range(2):
                        added = pack(t + b, b, (i * 2 + j // 2) * 16)
                    after(added, settled=True)
                    own_parts(t)
                    if not (isinstance(t, int) and t == 0):
                        list_rows(t - 2, (j - 2) % GT)

            turns(dve, pack_turn, T // GT, steps)
            list_rows(T - 2, GT - 2)

            dve.wait_ge(diag_in, 16)
            link(nc.vector.tensor_copy(diag[:, :], diag_i[:, :]))
            listed = adj_i_sb[:, 0, 0:T * S].bitcast(fp32).rearrange("p (t s) -> p t s", t=T)
            link(nc.vector.tensor_scalar(listed, rows[:, :, 2:OWN].bitcast(fp32), 1.0, None, ALU.is_ge))
            link(nc.vector.tensor_reduce(deg[:, :], listed, AX.X, ALU.add))
            nc.vector.tensor_copy(deg[:, 0:1], deg[:, 0:1]).then_inc(deg_ready, 1)
            link(nc.vector.tensor_tensor(bad[:, 0, :], row_sum[:, :], diag[:, :], ALU.subtract))
            link(nc.vector.tensor_tensor(bad[:, 0, :], bad[:, 0, :], deg[:, :], ALU.not_equal))
            link(nc.vector.scalar_tensor_tensor(bad[:, 1, :], diag[:, :], -1.0, diag[:, :], ALU.add, ALU.mult))
            dve.wait_ge(off_ready, 1)
            nc.vector.tensor_copy(rows[:, :, 0], row_no1[:, :].to_broadcast([P, T]))
            nc.vector.tensor_copy(rows[:, :, 1], bank[6][:, 0:T])
            link(nc.vector.tensor_tensor(last[:, :], bank[6][:, 0:T], deg[:, :], ALU.add))
            link(nc.vector.tensor_scalar(bad[:, 2, :], last[:, :], float(E), None, ALU.is_gt))
            link(nc.vector.tensor_reduce(bad_col[:, :], bad[:, :, :].rearrange("p a t -> p (a t)"), AX.X, ALU.add))
            nc.vector.tensor_scalar(bad_col[:, :], bad_col[:, :], 1.0, None, ALU.min).then_inc(bad_rows, 1)
            dve.wait_ge(bad_sum, 1)
            nc.vector.tensor_scalar(bad_int[:, :], bank[6][0:1, 0:1], 1.0, None, ALU.min).then_inc(flag_ready, 1)
            link(nc.vector.scalar_tensor_tensor(minus_mid[:, :], deg[:, :], 0.5, last[:, :], ALU.mult, ALU.subtract))
            link(nc.vector.tensor_scalar(minus_mid[:, :], minus_mid[:, :], 0.5, None, ALU.add))
            nc.vector.scalar_tensor_tensor(reach[:, :], deg[:, :], 0.25, deg[:, :], ALU.mult, ALU.mult)\
              .then_inc(spans_ready, 1)
            dve.wait_ge(spans_ready, 1)

            def own_edges(t, j):
                dve.wait_ge(dist_ready, t + 1)
                nc.vector.tensor_scalar(row_to_edge[j], edge_dist, reach[:, bass.ds(t, 1)], None,
                                        ALU.is_lt).then_inc(rte_ready, 1)

            taken = bank[0][:, 0:C * NA].rearrange("p (c n) -> p c n", c=C)

            def take_places(t, j):
                wait(dve, etr_ready, t - 1)
                dve.wait_ge(edge_rows_ready, t + 1)
                nc.vector.tensor_scalar(minus_row[j % 2][:, :], taken[:, :, 0], -1.0, None, ALU.mult)
                nc.vector.tensor_copy(own_at_edge[j][:, :, :], taken[:, :, OWN:OWN + H])
                return mark(nc.vector.tensor_tensor(slot[:, :], edge_no[:, :], taken[:, :, 1], ALU.subtract))

            def find_slots(j):
                nc.vector.tensor_tensor(own_at_edge[j][:, :, :], own_at_edge[j][:, :, :], taken[:, :, OWN + H:NA], ALU.add)
                return mark(nc.vector.tensor_tensor(slot_is[j][:, :, :], iota_s[:, :, :],
                                                    slot[:, :].unsqueeze(2).to_broadcast([P, C, S]), ALU.is_equal))

            def take_neighbours(j):
                nc.vector.tensor_tensor(nb_sel[:, :, :], slot_is[j][:, :, :], taken[:, :, 2:OWN], ALU.mult)\
                  .then_inc(edge_rows_read, 1)

            def add_neighbours(t):
                dve.wait_ge(edge_rows_read, t + 1)
                return mark(nc.vector.tensor_reduce(nb_f[:, :], nb_sel[:, :, :], AX.X, ALU.add))

            def index_neighbours(j):
                nc.vector.tensor_scalar(nb_idx[j % 2][:, :], nb_f[:, :], -1.0, float(N), ALU.mult,
                                        ALU.add).then_inc(nb_ready, 1)

            def multiply(t, j, n_in):
                for c in range(0, C, 2):
                    m = min(2, C - c)
                    dve.wait_ge(q_edges, t * 3 + (c // 2 + 1))
                    for i in range(m):
                        dve.wait_ge(nb_in[j][c + i], n_in)
                    nc.vector.tensor_tensor(prod[:, c:c + m, :],
                                            bank[2 + c // 2][:, 0:m * D].rearrange("p (c n) -> p c n", c=m),
                                            kv_e[j][:, c:c + m, 0:D], ALU.mult).then_inc(q_edges_read, 1)

            def add_products(t):
                dve.wait_ge(q_edges_read, t * 3 + 3)
                return mark(nc.vector.tensor_reduce(score[:, :, :].rearrange("p c h -> p (c h)"),
                                                    prod[:, :, :].rearrange("p c (h d) -> p (c h) d", d=DK), AX.X, ALU.add))

            def into_slots(t, j):
                link(nc.vector.tensor_tensor(score_d[:, :, :], score[:, :, :], own_at_edge[j][:, :, :], ALU.subtract))
                nc.vector.tensor_tensor(spread[:, :, :, :], score_d[:, :, :].unsqueeze(2).to_broadcast([P, C, S, H]),
                                        slot_is[j][:, :, :].unsqueeze(3).to_broadcast([P, C, S, H]),
                                        ALU.mult).then_inc(slots_ready, 1)

            def maximum(t):
                dve.wait_ge(slots_filled, t + 1)
                link(nc.vector.tensor_reduce(top_raw[:, :], bank[1][:, 0:S * H].rearrange("p (s h) -> p h s", s=S),
                                             AX.X, ALU.max))
                nc.vector.tensor_scalar(top_parts[:, 0, :], top_raw[:, :], 0.0, None, ALU.max)
                link(nc.vector.tensor_scalar(top[:, :], top_raw[:, :], 0.0, None, ALU.max))
                nc.vector.tensor_tensor(top_parts[:, 1, :], top[:, :], top_parts[:, 0, :].bitcast(fp32),
                                        ALU.subtract).then_inc(top_ready, 1)

            def below_maximum(t):
                dve.wait_ge(top_spread, t + 1)
                parts = bank[1][:, 0:C * 2 * H].rearrange("p (c i h) -> p c i h", c=C, i=2)
                link(nc.vector.tensor_tensor(score_m[:, :, :], score_d[:, :, :], parts[:, :, 0, :], ALU.subtract))
                nc.vector.tensor_tensor(score_m[:, :, :], score_m[:, :, :], parts[:, :, 1, :],
                                        ALU.subtract).then_inc(shifted, 1)

            def weigh_values(t, j, n_in):
                dve.wait_ge(own_in[j], n_in)
                dve.wait_ge(weights_ready, t + 1)
                nc.vector.tensor_tensor(pv[:, :, 0:D].rearrange("p c (h d) -> p c h d", h=H),
                                        kv_e[j][:, :, D:2 * D].rearrange("p c (h d) -> p c h d", h=H),
                                        pv[:, :, D:D + H].unsqueeze(3).to_broadcast([P, C + 1, H, DK]),
                                        ALU.mult).then_inc(pv_ready, 1)

            def normalise(t, j):
                dve.wait_ge(pv_ready, t + 1)
                dve.wait_ge(ctx_summed, t + 1)
                link(nc.vector.tensor_tensor(ctx_acc[:, :], bank[5][:, 0:D + H], pv[:, C, :], ALU.add))
                link(nc.vector.reciprocal(inv_den[:, :], ctx_acc[:, D:D + H]))
                nc.vector.tensor_tensor(att[:, j, :].rearrange("p (h d) -> p h d", h=H),
                                        ctx_acc[:, 0:D].rearrange("p (h d) -> p h d", h=H),
                                        inv_den[:, :].unsqueeze(2).to_broadcast([P, H, DK]),
                                        ALU.mult).then_inc(att_ready, 1)

            def h1_bias(u, k):
                wait(dve, ff2_read, (u - 1) * GT + (k + 1))
                dve.wait_ge(h1_ready, u * GT + (k + 1))
                nc.vector.tensor_tensor(h1_b2[k], h1[k], b2_sb[:, :], ALU.add).then_inc(h1_b2_ready, 1)

            def measure(ln, h_sum):
                return mark(nc.vector.bn_stats(stats[ln][:, :], h_sum))

            def mean_and_variance(ln):
                return mark(nc.vector.bn_aggr(mean_var[ln][:, :], stats[ln][:, :]))

            def moments(ln):
                nc.vector.tensor_scalar(mean_var[ln][:, 0:1], mean_var[ln][:, 0:1], -1.0, None, ALU.mult)
                nc.vector.tensor_scalar(mean_var[ln][:, 1:2], mean_var[ln][:, 1:2], EPS, None, ALU.add)\
                  .then_inc(var_ready[ln], 1)

            def first_sum(n, j):
                dve.wait_ge(x_bo_ready, n + 1)
                dve.wait_ge(proj_ready, n + 1)
                wait(dve, h1_ready, n)
                nc.vector.tensor_tensor(h_sum1, bank[6][:, 0:D], x_res[j], ALU.add).then_inc(res_added, 1)

            def first_moments(n):
                settled_wait(dve, res_added, n + 1)
                after(measure(0, h_sum1), settled=True)
                after(mean_and_variance(0))
                moments(0)

            def second_sum(u, k):
                n = u * GT + k
                dve.wait_ge(h1_b2_ready, n + 1)
                dve.wait_ge(ff2_ready, n + 1)
                wait(dve, y_out[k], u * 16)
                nc.vector.tensor_tensor(y[k], bank[7 - k % 2][:, 0:D], h1_b2[k], ALU.add).then_inc(ff2_read, 1)

            def second_moments(u, k):
                settled_wait(dve, ff2_read, u * GT + (k + 1))
                wait(dve, rstd_ready[1], u * GT + k)
                after(measure(1, y[k]), settled=True)
                after(mean_and_variance(1))
                moments(1)

            def slot_work(turn, j):
                s = turn * GT + j
                ahead, scored, summed, projected = (exists(s + n) for n in (2, 0, -1, -2))
                if scored:
                    multiply(s, j, turn * 16 + 16)
                finished = exists((turn - 2) * GT) and j in (1, 2)
                if scored:
                    products = add_products(s)
                if summed:
                    weigh_values(s - 1, (j - 1) % GT, (turn - (j == 0)) * 16 + 16)
                if scored:
                    after(products)
                    into_slots(s, j)
                if finished:
                    second_sum(turn - 2, 2 * j - 2)
                if ahead:
                    own_edges(s + 2, (j + 2) % GT)
                if finished:
                    second_sum(turn - 2, 2 * j - 1)
                    second_moments(turn - 2, 2 * j - 2)
                if isinstance(turn, int) and turn == 1 and j == 1:
                    dve.wait_ge(consts_in, CONSTS_IN)
                if exists((turn - 1) * GT) and j in (1, 2):
                    for k in (2 * j - 2, 2 * j - 1):
                        h1_bias(turn - 1, k)
                if scored:
                    maximum(s)
                if ahead:
                    placed_at = take_places(s + 2, (j + 2) % GT)
                    after(placed_at)
                    found_at = find_slots((j + 2) % GT)
                if projected:
                    first_sum(s - 2, (j - 2) % GT)
                if ahead:
                    after(found_at)
                    take_neighbours((j + 2) % GT)
                if projected:
                    settled_wait(dve, res_added, s - 1)
                    measured = measure(0, h_sum1)
                if ahead:
                    added = add_neighbours(s + 2)
                if projected:
                    after(measured, settled=True)
                    aggregated = mean_and_variance(0)
                if ahead:
                    after(added)
                    index_neighbours((j + 2) % GT)
                if projected:
                    after(aggregated)
                    moments(0)
                if finished:
                    second_moments(turn - 2, 2 * j - 1)
                if summed:
                    normalise(s - 1, (j - 1) % GT)
                if scored:
                    below_maximum(s)

            run_slots(dve, slot_work, steps)

            def dense():
                mask_steps, head_steps = counter(), counter()

                def mlink(ins):
                    ins.then_inc(mask_step, 1)
                    settled_wait(dve, mask_step, raised(mask_steps))

                def hlink(ins, settled=False):
                    ins.then_inc(dense_step, 1)
                    (settled_wait if settled else wait)(dve, dense_step, raised(head_steps))

                nc.vector.memset(top[:, 0:1], 0.0).then_inc(free_made, 1)
                nc.vector.memset(top[:, 1:2], 0.0).then_inc(kT_copied, 1)
                nc.vector.memset(top[:, 2:3], 0.0).then_inc(head_free, 1)
                with dve.Fori(0, T) as m:
                    dve.wait_ge(kT_ps, m + 1)
                    nc.vector.tensor_copy(d_kT_out, bank[0][:, 0:KD * P].rearrange("p (k n) -> p k n", k=KD))\
                        .then_inc(kT_copied, 1)
                with dve.Fori(0, G) as g:
                    with dve.Fori(0, GT) as j:
                        t = g * GT + j
                        enter(mask_steps, t, 0, 2)
                        dve.wait_ge(mask_in, t * 16 + 16)
                        mlink(nc.vector.scalar_tensor_tensor(d_junk[:, :], d_mask[:, bass.ds(t * P, P)], -1.0,
                                                             ident[:, :], ALU.mult, ALU.not_equal))
                        mlink(nc.vector.tensor_copy(d_mask[:, bass.ds(t * P, P)], d_junk[:, :]))
                        with dve.Fori(0, H) as h:
                            n = t * H + h
                            enter(head_steps, n, 0, 5)
                            nc.vector.tensor_copy(d_q, q_sb[:, bass.ds(t, 1), bass.ds(h * DK, DK)]
                                                  .rearrange("p o n -> p (o n)")).then_inc(head_q, 1)
                            dve.wait_ge(qT_ps, n + 1)
                            nc.vector.tensor_copy(d_qT, bank[0][0:DK, 0:P]).then_inc(qT_ready, 1)
                            hlink(nc.vector.memset(d_score, -1e9 / SCALE), settled=True)
                            for c in range(NS):
                                settled_wait(dve, scores_ps, n * NS + (c + 1))
                                nc.vector.copy_predicated(d_score[:, c * SC:(c + 1) * SC], d_mask[:, c * SC:(c + 1) * SC],
                                                          bank[2 + c % 2][:, :]).then_inc(scores_kept, 1)
                            dve.wait_ge(scores_kept, n * NS + NS)
                            hlink(nc.vector.tensor_reduce(d_max, d_score, AX.X, ALU.max))
                            nc.vector.tensor_scalar(d_shift, d_max, -SCALE, None, ALU.mult).then_inc(shift_ready, 1)
                            dve.wait_ge(head_summed, n + 1)
                            hlink(nc.vector.reciprocal(d_inv, d_den))
                            hlink(nc.vector.tensor_scalar(att[:, bass.ds(j, 1), bass.ds(h * DK, DK)]
                                                          .rearrange("p o n -> p (o n)"), bank[5][:, 0:DK], d_inv, None,
                                                          ALU.mult))
                            hlink(nc.vector.memset(d_max, 0.0))
                            nc.vector.memset(d_max, 0.0).then_inc(head_free, 1)
                        nc.vector.memset(inv_den[:, 4:5], 0.0).then_inc(att_ready, 1)
                        leave(mask_steps, 0)
                        leave(head_steps, 0)
                    u = g + G
                    enter(steps, g, 0, 2 * GT * LN_LINKS)
                    for k in range(GT):
                        first_sum(u * GT + k, k)
                        first_moments(u * GT + k)
                    for k in range(GT):
                        h1_bias(u, k)
                    for k in range(GT):
                        second_sum(u, k)
                        second_moments(u, k)
                    leave(steps, G)

            if_dense(dve, dense)

        @block.tensor
        def _(pe):
            pe.wait_ge(qkv_in, QKV_IN)
            pe.wait_ge(consts_made, CONSTS)

            def pack_turn(i):
                for half in range(2):
                    for b in range(2):
                        t = i * GT + half * 2 + b
                        pe.wait_ge(xT_in[b], (i * 2 + half) * 16 + 16)
                        wait(pe, q_ready, t - 1)
                        for k in range(KD):
                            nc.tensor.matmul(bank[b][:, :], xT_sb[b][:, k, :], wkv_sb[:, k, :], start=k == 0, stop=k == KD - 1)
                        for k in range(KD):
                            ins = nc.tensor.matmul(bank[2 + b][:, 0:D], xT_sb[b][:, k, :], wq_sb[:, k, :],
                                                   start=k == 0, stop=k == KD - 1)
                        ins.then_inc(qkv_ready, 1)
                    for b in range(2):
                        t, j = i * GT + half * 2 + b, half * 2 + b
                        pe.wait_ge(diag_cleared, t + 1)
                        for a in range(A):
                            nc.tensor.matmul(bank[4 + j][:, 0:B], bit_diag[:, a, :],
                                             adj_b[b][:, (A - 1 - a) * B:(A - a) * B], start=a == 0, stop=False)
                        nc.tensor.matmul(bank[4 + j][:, 0:B], bit_diag[:, A, :], word_no[:, :],
                                         start=False, stop=True).then_inc(words_ready, 1)

            turns(pe, pack_turn, T // GT)

            pe.wait_ge(deg_ready, 1)
            nc.tensor.matmul(bank[6][:, 0:T], before[:, :], deg[:, :], start=True, stop=True).then_inc(off_ready, 1)
            pe.wait_ge(bad_rows, 1)
            nc.tensor.matmul(bank[6][0:1, 0:1], bad_col[:, :], ones_col[:, :], start=True, stop=True).then_inc(bad_sum, 1)

            def to_edges(j, width, psum, what):
                for c in range(C):
                    ins = nc.tensor.matmul(psum[:, c * width:(c + 1) * width], row_to_edge[j][:, c * P:(c + 1) * P],
                                           what, start=True, stop=True)
                return ins

            def keep_busy(count):
                for _ in range(count):
                    nc.tensor.matmul(bank[7][:, :], ident[:, :], iota_e[:, 0:512], start=True, stop=True)

            def edges(t, j):
                pe.wait_ge(rte_ready, t + 1)
                wait(pe, edge_rows_read, t)
                to_edges(j, NA, bank[0], rows[:, bass.ds(t, 1), :].rearrange("p o n -> p (o n)"))\
                    .then_inc(edge_rows_ready, 1)

            def queries(t, j):
                pe.wait_ge(q_split, t + 1)
                for c in range(C):
                    if c % 2 == 0:
                        wait(pe, q_edges_read, (t - 1) * 3 + (c // 2 + 1))
                    for i in range(2):
                        ins = nc.tensor.matmul(bank[2 + c // 2][:, c % 2 * D:c % 2 * D + D],
                                               row_to_edge[j][:, c * P:(c + 1) * P], q_parts[:, i, :],
                                               start=i == 0, stop=i == 1)
                    if c % 2 == 1 or c == C - 1:
                        ins.then_inc(q_edges, 1)

            def fill_slots(t, j):
                pe.wait_ge(slots_ready, t + 1)
                pe.wait_ge(etr_ready, t + 1)
                wait(pe, shifted, t)
                for c in range(C):
                    ins = nc.tensor.matmul(bank[1][:, 0:S * H], edge_to_row[j % 2][:, c, :],
                                           spread[:, c, :, :].rearrange("p s h -> p (s h)"), start=c == 0, stop=c == C - 1)
                ins.then_inc(slots_filled, 1)

            def spread_top(t, j):
                pe.wait_ge(top_ready, t + 1)
                to_edges(j, 2 * H, bank[1], top_parts[:, :, :].rearrange("p i h -> p (i h)")).then_inc(top_spread, 1)

            def sum_values(t, j):
                pe.wait_ge(pv_ready, t + 1)
                wait(pe, att_ready, t)
                for c in range(C):
                    ins = nc.tensor.matmul(bank[5][:, 0:D + H], edge_to_row[j % 2][:, c, :], pv[:, c, :],
                                           start=c == 0, stop=c == C - 1)
                ins.then_inc(ctx_summed, 1)

            def turn_att(n, j):
                pe.wait_ge(att_ready, n + 1)
                wait(pe, res_added, n)
                for k in range(KD):
                    ins = nc.tensor.transpose(bank[6][:, k * P:(k + 1) * P], att[:, j, k * P:(k + 1) * P], ident[:, :])
                ins.then_inc(attT_ps, 1)

            def project(n):
                pe.wait_ge(attT_ready, n + 1)
                for k in range(KD):
                    ins = nc.tensor.matmul(bank[6][:, 0:D], attT[:, k, :], wo_sb[:, k, :], start=k == 0, stop=k == KD - 1)
                ins.then_inc(proj_ready, 1)

            def turn_h1(u, k):
                pe.wait_ge(h1_ready, u * GT + GT)
                for i in range(GT):
                    ins = nc.tensor.transpose(bank[7][:, i * P:(i + 1) * P], h1[i][:, k * P:(k + 1) * P], ident[:, :])
                ins.then_inc(h1T_ps, 1)

            def ff1(u, f):
                pe.wait_ge(h1T_ready, u * KD + KD)
                wait(pe, hidden_ready, u * KF + (f - 1))
                for k in range(KD):
                    ins = nc.tensor.matmul(bank[7 - f % 2][:, :], w1_sb[:, k, f * P:(f + 1) * P], h1T[:, k, :],
                                           start=k == 0, stop=k == KD - 1)
                ins.then_inc(ff1_ready, 1)

            def ff2(u, k):
                pe.wait_ge(hidden_ready, u * KF + KF)
                if k >= 2:
                    pe.wait_ge(ff2_read, u * GT + (k - 1))
                for f in range(KF):
                    ins = nc.tensor.matmul(bank[7 - k % 2][:, 0:D], uT[:, f, k * P:(k + 1) * P], w2_sb[:, f, :],
                                           start=f == 0, stop=f == KF - 1)
                ins.then_inc(ff2_ready, 1)

            def slot(turn, j):
                s = turn * GT + j
                if isinstance(turn, int) and s == 2:
                    pe.wait_ge(consts_in, CONSTS_IN)
                behind, before_it = exists((turn - 1) * GT), exists((turn - 2) * GT)
                if before_it and j == 0:
                    ff1(turn - 2, 6)
                    ff1(turn - 2, 7)
                if before_it and j in (1, 2):
                    if exists(s - 3):
                        pe.wait_ge(res_added, s - 2)
                    ff2(turn - 2, 2 * j - 1)
                if behind and j == 3:
                    ff1(turn - 1, 2)
                if behind and j == 2:
                    wait(pe, ff2_read, (turn - 2) * GT + 3)
                    turn_h1(turn - 1, 0)
                if isinstance(turn, int) and -1 <= s < GT + 2:
                    keep_busy(5)
                if exists(s):
                    fill_slots(s, j)
                if behind and j == 2:
                    pe.wait_ge(h1T_ready, (turn - 1) * KD + 1)
                    turn_h1(turn - 1, 1)
                if exists(s - 2):
                    wait(pe, *((hidden_ready, (turn - 2) * KF + 8), (ff2_read, (turn - 2) * GT + 2),
                               (ff2_read, (turn - 2) * GT + 4), (hidden_ready, (turn - 1) * KF + 2))[j])
                    turn_att(s - 2, (j - 2) % GT)
                if exists(s + 2):
                    edges(s + 2, (j + 2) % GT)
                if exists(s - 2):
                    project(s - 2)
                if exists(s - 1):
                    sum_values(s - 1, (j - 1) % GT)
                if exists(s):
                    spread_top(s, j)
                if exists(s + 1):
                    queries(s + 1, (j + 1) % GT)
                if before_it and j < 2:
                    ff2(turn - 2, 2 * j)
                if behind and j == 2:
                    ff1(turn - 1, 0)
                if behind and j >= 2:
                    if exists(s - 2):
                        pe.wait_ge(res_added, s - 1)
                    if j == 2:
                        wait(pe, ff2_read, (turn - 2) * GT + 4)
                        ff1(turn - 1, 1)
                    else:
                        for f in (3, 4, 5):
                            ff1(turn - 1, f)

            run_slots(pe, slot)

            def dense():
                with pe.Fori(0, T) as m:
                    pe.wait_ge(k_rows_in, m * 16 + 16)
                    for k in range(KD):
                        ins = nc.tensor.transpose(bank[0][:, k * P:(k + 1) * P], d_k_rows[:, k * P:(k + 1) * P], ident[:, :])
                    ins.then_inc(kT_ps, 1)
                with pe.Fori(0, G) as g:
                    with pe.Fori(0, GT) as j:
                        with pe.Fori(0, H) as h:
                            n = (g * GT + j) * H + h
                            pe.wait_ge(head_q, n + 1)
                            nc.tensor.transpose(bank[0][0:DK, 0:P], d_q, ident[:, :]).then_inc(qT_ps, 1)
                            pe.wait_ge(qT_ready, n + 1)
                            pe.wait_ge(head_in, n * 32 + 32)
                            for c in range(NS):
                                if c >= 2:
                                    pe.wait_ge(scores_kept, n * NS + (c - 1))
                                nc.tensor.matmul(bank[2 + c % 2][:, :], d_qT, d_kT[:, c * SC:(c + 1) * SC],
                                                 start=True, stop=True).then_inc(scores_ps, 1)
                            pe.wait_ge(probs_ready, n + 1)
                            for m in range(M4 + 1):
                                if m < M4:
                                    if m >= 2:
                                        pe.wait_ge(pT_ready, n * M4 + (m - 1))
                                    for i in range(4):
                                        ins = nc.tensor.transpose(bank[m % 2][:, i * P:(i + 1) * P],
                                                                  d_score[:, (m * 4 + i) * P:(m * 4 + i + 1) * P], ident[:, :])
                                    ins.then_inc(pT_ps, 1)
                                if m >= 1:
                                    pe.wait_ge(pT_ready, n * M4 + m)
                                    for i in range(4):
                                        c = (m - 1) * 4 + i
                                        ins = nc.tensor.matmul(bank[5][:, 0:DK], d_pT[(m - 1) % 2][:, i * P:(i + 1) * P],
                                                               d_v[:, c, :], start=c == 0, stop=c == T - 1)
                            ins.then_inc(head_summed, 1)
                    u = g + G
                    pe.wait_ge(ff2_read, u * GT)
                    for k in range(GT):
                        turn_att(u * GT + k, k)
                        project(u * GT + k)
                    pe.wait_ge(res_added, u * GT + GT)
                    for k in range(KD):
                        if k > 0:
                            pe.wait_ge(h1T_ready, u * KD + k)
                        turn_h1(u, k)
                    for f in range(KF):
                        ff1(u, f)
                    for k in range(GT):
                        ff2(u, k)

            if_dense(pe, dense)


def kernel(x, adj, L0_gnn_Wq, L0_gnn_bq, L0_gnn_Wk, L0_gnn_bk, L0_gnn_Wv, L0_gnn_bv, L0_gnn_Wo, L0_gnn_bo, L0_gnn_W1,
           L0_gnn_b1, L0_gnn_W2, L0_gnn_b2, L0_gnn_ln1_g, L0_gnn_ln1_b, L0_gnn_ln2_g, L0_gnn_ln2_b):
    import numpy as np
    import concourse.bacc as bacc
    from concourse.bass_utils import run_bass_kernel_spmd

    laid_out = {
        "x": x, "xT": np.asarray(x).T, "adj": adj, "wqT": np.asarray(L0_gnn_Wq).T, "wkT": np.asarray(L0_gnn_Wk).T,
        "wvT": np.asarray(L0_gnn_Wv).T, "woT": np.asarray(L0_gnn_Wo).T, "w1T": np.asarray(L0_gnn_W1).T,
        "w2T": np.asarray(L0_gnn_W2).T, "bq": L0_gnn_bq, "bk": L0_gnn_bk, "bv": L0_gnn_bv, "bo": L0_gnn_bo,
        "b1": L0_gnn_b1, "b2": L0_gnn_b2, "ln1_g": L0_gnn_ln1_g, "ln1_b": L0_gnn_ln1_b, "ln2_g": L0_gnn_ln2_g,
        "ln2_b": L0_gnn_ln2_b,
    }
    arrays = {f"in_{name}": np.ascontiguousarray(a) for name, a in laid_out.items()}
    nc = bacc.Bacc("TRN2", target_bir_lowering=False, num_devices=1)
    aps = [nc.dram_tensor(name, a.shape, mybir.dt.from_np(a.dtype), kind="ExternalInput").ap() for name, a in arrays.items()]
    out = nc.dram_tensor("out_h", arrays["in_x"].shape, mybir.dt.float32, kind="ExternalOutput").ap()
    graph_attention_kernel(nc, *aps, out)
    result = run_bass_kernel_spmd(nc, [arrays], core_ids=[0])
    return result.results[0]["out_h"]
```
